# Optimizing a Trainium2 kernel written in Bass

```python
import numpy as np
import jax
import jax.numpy as jnp

def _softmax(x, axis=-1):
    return jax.nn.softmax(x, axis=axis)

def _gelu(x):
    return jax.nn.gelu(x, approximate=True)

def _silu(x):
    return jax.nn.silu(x)

def _sigmoid(x):
    return jax.nn.sigmoid(x)

def _layernorm(x, axis=-1, eps=1e-05):
    m = jnp.mean(x, axis=axis, keepdims=True)
    v = jnp.var(x, axis=axis, keepdims=True)
    return (x - m) / jnp.sqrt(v + eps)

def _scatter_add(tgt, idx, src, axis=0):
    return tgt.at[idx].add(src)

def _segment_sum(src, seg, n):
    return jax.ops.segment_sum(src, seg, n)
kernel_name = 'mk_cond_resid_d4_seqx_r4_c2c545'

def setup_inputs(seed: int=0):
    np.random.seed(seed)
    _w = jnp.asarray

    def _rec_inputs():
        import jax
        import jax.numpy as jnp
        _rk = jax.random.key(seed)
        x = -0.0003929 + 0.9999 * jax.random.normal(jax.random.fold_in(_rk, 1), (16, 256, 256), jnp.float32)
        _lenS = 256 - jax.random.randint(jax.random.fold_in(_rk, 7), (16,), 0, max(1, 256 // 4) + 1, jnp.int32)
        _lenS2 = 256 - jax.random.randint(jax.random.fold_in(_rk, 8), (16,), 0, max(1, 256 // 4) + 1, jnp.int32)
        itok_B_0_7 = jax.random.randint(jax.random.fold_in(_rk, 11), (16,), 0, 8, jnp.int32)
        itok_B_0_2 = jax.random.randint(jax.random.fold_in(_rk, 12), (16,), 0, 3, jnp.int32)
        itok_B_1_98 = jax.random.randint(jax.random.fold_in(_rk, 13), (16,), 1, 99, jnp.int32)
        return (x, itok_B_0_7, itok_B_0_2, itok_B_1_98)
    x, itok_B_0_7, itok_B_0_2, itok_B_1_98 = _rec_inputs()

    def _L0_cond_setup():
        import jax, jax.numpy as jnp
        import numpy as np
        B, S, D, F = (32, 128, 256, 1024)
        R_COMMON, R_DOMAIN, E = (16, 16, 8)
        ALPHA = 2.0

        def _expert_lora(x, expert_ids, Wa, Wb):
            Ab = Wa[expert_ids]
            Bb = Wb[expert_ids]
            low = jnp.einsum('bsd,brd->bsr', x, Ab)
            return ALPHA * jnp.einsum('bsr,bor->bso', low, Bb)
        key = jax.random.key(seed)
        ks = jax.random.split(key, 12)
        sd = lambda k, shape: jax.random.normal(k, shape, dtype=jnp.float32) * (1.0 / np.sqrt(shape[-1]))
        return {'hidden_states': jax.random.normal(ks[0], (B, S, D), dtype=jnp.float32), 'expert_ids': jax.random.randint(ks[1], (B,), 0, E, dtype=jnp.int32), 'wi': sd(ks[2], (F, D)), 'wo': sd(ks[3], (D, F)), 'common_wi_a': sd(ks[4], (R_COMMON, D)), 'common_wi_b': sd(ks[5], (F, R_COMMON)), 'common_wo_a': sd(ks[6], (R_COMMON, F)), 'common_wo_b': sd(ks[7], (D, R_COMMON)), 'experts_wi_a': sd(ks[8], (E, R_DOMAIN, D)), 'experts_wi_b': sd(ks[9], (F, R_DOMAIN)) * jnp.ones((E, 1, 1)) * 0.0 + sd(ks[9], (E, F, R_DOMAIN)), 'experts_wo_a': sd(ks[10], (E, R_DOMAIN, F)), 'experts_wo_b': sd(ks[11], (E, D, R_DOMAIN))}
    _L0_cond_all = _L0_cond_setup()
    _L0_cond_in = {k: v for k, v in _L0_cond_all.items() if k in ('wi', 'wo', 'common_wi_a', 'common_wi_b', 'common_wo_a', 'common_wo_b', 'experts_wi_a', 'experts_wi_b', 'experts_wo_a', 'experts_wo_b')}
    del _L0_cond_all

    def _L1_cond_setup():
        import jax, jax.numpy as jnp
        import numpy as np
        NEG_INF = -1e+30
        key = jax.random.key(seed)
        k1, k2, k3, k4, k5 = jax.random.split(key, 5)
        B, S, D, A = (16, 256, 256, 64)
        hidden = jax.random.normal(k1, (B, S, D), dtype=jnp.float32)
        W1 = jax.random.normal(k2, (D, A), dtype=jnp.float32) / np.sqrt(D)
        b1 = jax.random.normal(k3, (A,), dtype=jnp.float32) * 0.01
        v = jax.random.normal(k4, (A,), dtype=jnp.float32) / np.sqrt(A)
        prompt_type_ids = jax.random.randint(k5, (B,), 0, 3, dtype=jnp.int32)
        return {'hidden': hidden, 'W1': W1, 'b1': b1, 'v': v, 'prompt_type_ids': prompt_type_ids}
    _L1_cond_all = _L1_cond_setup()
    _L1_cond_in = {k: v for k, v in _L1_cond_all.items() if k in ('W1', 'b1', 'v')}
    del _L1_cond_all

    def _L2_cond_setup():
        import jax, jax.numpy as jnp
        import numpy as np
        S, O, H = (8, 256, 256)
        B, N = (32, 128)
        key = jax.random.key(seed)
        k1, k2, k3, k4 = jax.random.split(key, 4)
        x = jax.random.normal(k1, (B, N, H), dtype=jnp.float32)
        subject_id = jax.random.randint(k2, (B,), 0, S)
        wbound = jnp.sqrt(2.0 / 6.0) * jnp.sqrt(3.0 / H)
        weight = jax.random.uniform(k3, (S, O, H), minval=-wbound, maxval=wbound, dtype=jnp.float32)
        bbound = 1.0 / jnp.sqrt(H)
        bias = jax.random.uniform(k4, (S, O), minval=-bbound, maxval=bbound, dtype=jnp.float32)
        return {'x': x, 'subject_id': subject_id, 'weight': weight, 'bias': bias}
    _L2_cond_all = _L2_cond_setup()
    _L2_cond_in = {k: v for k, v in _L2_cond_all.items() if k in ('weight', 'bias')}
    del _L2_cond_all

    def _L3_cond_setup():
        import jax, jax.numpy as jnp
        import numpy as np
        B = 128
        D = 256
        K = 100
        key = jax.random.key(seed)
        kx, kt, ks = jax.random.split(key, 3)
        x = jax.random.normal(kx, (B, D, D), dtype=jnp.float32)
        T = jax.random.normal(kt, (K, D, D), dtype=jnp.float32)
        fwd_steps = jax.random.randint(ks, (B,), 1, K + 1, dtype=jnp.int64)
        return {'x': x, 'fwd_steps': fwd_steps, 'T': T}
    _L3_cond_all = _L3_cond_setup()
    _L3_cond_in = {k: v for k, v in _L3_cond_all.items() if k in ('T',)}
    del _L3_cond_all
    return {'x': x, 'itok_B_0_7': itok_B_0_7, 'itok_B_0_2': itok_B_0_2, 'itok_B_1_98': itok_B_1_98, 'L0_cond_wi': _L0_cond_in['wi'], 'L0_cond_wo': _L0_cond_in['wo'], 'L0_cond_common_wi_a': _L0_cond_in['common_wi_a'], 'L0_cond_common_wi_b': _L0_cond_in['common_wi_b'], 'L0_cond_common_wo_a': _L0_cond_in['common_wo_a'], 'L0_cond_common_wo_b': _L0_cond_in['common_wo_b'], 'L0_cond_experts_wi_a': _L0_cond_in['experts_wi_a'], 'L0_cond_experts_wi_b': _L0_cond_in['experts_wi_b'], 'L0_cond_experts_wo_a': _L0_cond_in['experts_wo_a'], 'L0_cond_experts_wo_b': _L0_cond_in['experts_wo_b'], 'L1_cond_W1': _L1_cond_in['W1'], 'L1_cond_b1': _L1_cond_in['b1'], 'L1_cond_v': _L1_cond_in['v'], 'L2_cond_weight': _L2_cond_in['weight'], 'L2_cond_bias': _L2_cond_in['bias'], 'L3_cond_T': _L3_cond_in['T']}

def reference(x, itok_B_0_7, itok_B_0_2, itok_B_1_98, L0_cond_wi, L0_cond_wo, L0_cond_common_wi_a, L0_cond_common_wi_b, L0_cond_common_wo_a, L0_cond_common_wo_b, L0_cond_experts_wi_a, L0_cond_experts_wi_b, L0_cond_experts_wo_a, L0_cond_experts_wo_b, L1_cond_W1, L1_cond_b1, L1_cond_v, L2_cond_weight, L2_cond_bias, L3_cond_T):
    import jax
    import jax.numpy as jnp

    def _L0_cond_ref(hidden_states, expert_ids, wi, wo, common_wi_a, common_wi_b, common_wo_a, common_wo_b, experts_wi_a, experts_wi_b, experts_wo_a, experts_wo_b):
        import jax, jax.numpy as jnp
        import numpy as np
        B, S, D, F = (32, 128, 256, 1024)
        R_COMMON, R_DOMAIN, E = (16, 16, 8)
        ALPHA = 2.0

        def _expert_lora(x, expert_ids, Wa, Wb):
            Ab = Wa[expert_ids]
            Bb = Wb[expert_ids]
            low = jnp.einsum('bsd,brd->bsr', x, Ab)
            return ALPHA * jnp.einsum('bsr,bor->bso', low, Bb)
        x = hidden_states
        hidden_i = jnp.einsum('bsd,fd->bsf', x, wi)
        hidden_i += ALPHA * jnp.einsum('bsr,fr->bsf', jnp.einsum('bsd,rd->bsr', x, common_wi_a), common_wi_b)
        hidden_i += _expert_lora(x, expert_ids, experts_wi_a, experts_wi_b)
        hidden_i = jax.nn.relu(hidden_i)
        hidden_o = jnp.einsum('bsf,df->bsd', hidden_i, wo)
        hidden_o += ALPHA * jnp.einsum('bsr,dr->bsd', jnp.einsum('bsf,rf->bsr', hidden_i, common_wo_a), common_wo_b)
        hidden_o += _expert_lora(hidden_i, expert_ids, experts_wo_a, experts_wo_b)
        return hidden_o

    def _L1_cond_ref(hidden, W1, b1, v, prompt_type_ids):
        import jax, jax.numpy as jnp
        import numpy as np
        NEG_INF = -1e+30
        B, S, D = hidden.shape
        attn_in = jnp.tanh(jnp.einsum('bsd,da->bsa', hidden, W1) + b1)
        scores = jnp.einsum('bsa,a->bs', attn_in, v)
        idx = jnp.arange(S)
        j = idx[:, None]
        l = idx[None, :]
        prefix_m = l <= j
        postfix_m = l >= j
        cloze_m = l != j
        pt = prompt_type_ids[:, None, None]
        mask = jnp.where(pt == 0, prefix_m[None], jnp.where(pt == 1, postfix_m[None], cloze_m[None]))
        masked_scores = jnp.where(mask, scores[:, None, :], NEG_INF)
        p = jax.nn.softmax(masked_scores, axis=-1)
        cnt = jnp.sum(mask, axis=-1).astype(hidden.dtype)
        pooled = jnp.einsum('bjl,bld->bjd', p, hidden) / cnt[..., None]
        return pooled

    def _L2_cond_ref(x, subject_id, weight, bias):
        import jax, jax.numpy as jnp
        import numpy as np
        S, O, H = (8, 256, 256)
        B, N = (32, 128)
        W = weight[subject_id]
        b = bias[subject_id]
        y = jnp.einsum('bnh,boh->bno', x, W) + b[:, None, :]
        return y

    def _L3_cond_ref(x, fwd_steps, T):
        import jax, jax.numpy as jnp
        import numpy as np
        B = 128
        D = 256
        K = 100
        Tb = T[fwd_steps - 1]
        return jnp.einsum('bij,bjk->bik', Tb, x)
    x = x + _L0_cond_ref(x, itok_B_0_7, L0_cond_wi, L0_cond_wo, L0_cond_common_wi_a, L0_cond_common_wi_b, L0_cond_common_wo_a, L0_cond_common_wo_b, L0_cond_experts_wi_a, L0_cond_experts_wi_b, L0_cond_experts_wo_a, L0_cond_experts_wo_b)
    x = x + _L1_cond_ref(x, L1_cond_W1, L1_cond_b1, L1_cond_v, itok_B_0_2)
    x = x + _L2_cond_ref(x, itok_B_0_7, L2_cond_weight, L2_cond_bias)
    x = x + _L3_cond_ref(x, itok_B_1_98, L3_cond_T)
    return x

_drawn_inputs = setup_inputs


def setup_inputs(seed=0):
    import zlib

    import numpy as np

    out = dict(_drawn_inputs(seed))
    spreads = {}
    factors = {'L1_cond_W1': 4.488, 'L1_cond_b1': 8.0, 'L1_cond_v': 3.929, 'L2_cond_bias': 8.0}
    for name, (base, spread) in spreads.items():
        noise = np.random.default_rng([zlib.crc32(name.encode()), seed]).standard_normal(out[name].shape)
        drawn = base * np.exp(spread * noise) if base else spread * noise
        out[name] = jnp.asarray(drawn.astype(out[name].dtype))
    for name, factor in factors.items():
        out[name] = (out[name] * factor).astype(out[name].dtype)
    return out
```

```python
from contextlib import ExitStack

import concourse.bass as bass
from concourse import mybir

F32 = mybir.dt.float32
F32R = mybir.dt.float32r
BF16 = mybir.dt.bfloat16
I32 = mybir.dt.int32
ALU = mybir.AluOpType
ACT = mybir.ActivationFunctionType

P = 128
BIG = 1.0e30
ALPHA = 2.0


def build(nc, x, expert_id, mask_id, step_id, wi, wo, cwi_a, cwi_b, cwo_a, cwo_b,
          ewi_a, ewi_b, ewo_a, ewo_b, W1, b1, v, W2, bias2, T, out):
    B, S, D = x.shape
    F = wi.shape[0]
    E, R, _ = ewi_a.shape
    A = W1.shape[1]
    ST, DT, FT = S // P, D // P, F // P
    PAIRS = B // 2
    N2 = 2 * S
    G = P // R
    assert (ST, DT, 2 * A, E * R, G) == (2, 2, P, P, 8)

    with ExitStack() as ctx:
        def sb(name, shape, dt=F32):
            return ctx.enter_context(nc.sbuf_tensor(name, shape, dt))

        def sem(name):
            return ctx.enter_context(nc.semaphore(name))

        ids = sb("ids", [1, 3, B], I32)
        ident = sb("ident", [P, P])
        wiT_h = sb("wiT_h", [P, DT, F], F32R)
        wiT_l = sb("wiT_l", [P, DT, F], F32R)
        woT_h = sb("woT_h", [P, FT, R + D + R], F32R)
        woT_l = sb("woT_l", [P, FT, R + D + R], F32R)
        ewoT_h = sb("ewoT_h", [P, FT, E * R], F32R)
        ewoT_l = sb("ewoT_l", [P, FT, E * R], F32R)
        w2T_h = sb("w2T_h", [P, E, DT, D], F32R)
        w2T_l = sb("w2T_l", [P, E, DT, D], F32R)
        w1_h = sb("w1_h", [P, DT, P], F32R)
        w1_l = sb("w1_l", [P, DT, P], F32R)
        v_h = sb("v_h", [P, P], F32R)
        v_l = sb("v_l", [P, P], F32R)
        b1_c = sb("b1_c", [P, 1])
        v_c = sb("v_c", [P, 1])
        mask_big = sb("mask_big", [P, 3, ST, S], BF16)
        cnt = sb("cnt", [P, 3, ST])
        cnt_i = sb("cnt_i", [P, 3, ST], I32)
        pre_at = sb("pre_at", [1, 3], I32)
        suf_at = sb("suf_at", [1, 3], I32)
        pre_max = sb("pre_max", [P, S + 1 + S])
        suf_max = sb("suf_max", [P, S + S + 1])

        raw = ExitStack()

        def rb(name, shape, dt=F32):
            return raw.enter_context(nc.sbuf_tensor(name, shape, dt))

        w2_raw = rb("w2_raw", [P, E, DT, D])
        wo_raw = rb("wo_raw", [P, DT, F])
        coa_raw = rb("coa_raw", [R, F])
        cob_raw = rb("cob_raw", [P, DT * R])
        cobT = rb("cobT", [R, D])
        ewoa_raw = rb("ewoa_raw", [P, F])
        ewob_raw = rb("ewob_raw", [P, E, DT * R])
        ewob_s = rb("ewob_s", [P, DT, E * R])
        w1_raw = rb("w1_raw", [P, DT, A])
        eob_st = rb("eob_st", [P, 2, D], F32R)
        eia_st = rb("eia_st", [P, E, DT, P], F32R)
        rb("fill", [P, 704])
        wi_raw = rb("wi_raw", [P, FT, D])
        cia_raw = rb("cia_raw", [R, D])
        cib_raw = rb("cib_raw", [P, FT * R])
        cibT = rb("cibT", [R, F])
        ewia_raw = rb("ewia_raw", [P, D])
        ewib_raw = rb("ewib_raw", [P, E, FT * R])
        ewib_s = rb("ewib_s", [P, FT, E * R])
        eib_st = rb("eib_st", [P, 2, F], F32R)
        raw.close()

        x1T_h = sb("x1T_h", [P, DT, N2], F32R)
        x1T_l = sb("x1T_l", [P, DT, N2], F32R)
        th = sb("th", [P, N2])
        tstk = sb("tstk", [P, N2], F32R)
        mix = sb("mix", [P, 2, ST, S])
        p_h = sb("p_h", [P, 2, ST, S], F32R)
        p_l = sb("p_l", [P, 2, ST, S], F32R)
        x1_h = sb("x1_h", [P, 2, ST, D + 2], F32R)
        x1_l = sb("x1_l", [P, 2, ST, D + 2], F32R)
        x2 = sb("x2", [P, 2, ST, D])
        t_raw = sb("t_raw", [P, 2, ST, S])
        tT_h = sb("tT_h", [P, 2, ST, S], F32R)
        tT_l = sb("tT_l", [P, 2, ST, S], F32R)
        hT_h = sb("hT_h", [P, FT, N2], F32R)
        hT_l = sb("hT_l", [P, FT, N2], F32R)
        x3_h, x3_l = p_h, p_l
        x0 = sb("x0", [P, 2, ST, D])
        x0T_h = sb("x0T_h", [P, DT, N2], F32R)
        x0T_l = sb("x0T_l", [P, DT, N2], F32R)
        eia = sb("eia", [P, 2, DT, P], F32R)
        eib = sb("eib", [P, 2, F], F32R)
        low = sb("low", [P, N2], F32R)
        eob = sb("eob", [4 * R, 2, D], F32R)
        low_o = sb("low_o", [P, 2 * ST, G, R])
        lowT = sb("lowT", [4 * R, 2 * ST, P], F32R)
        x1 = sb("x1", [P, 2, ST, D])
        bias_t = sb("bias_t", [P, 2, D])
        mrow = sb("mrow", [P, S])
        s_col = sb("s_col", [P, 2 * ST, 2])
        zc = sb("zc", [P, 2 * ST])
        rz = sb("rz", [P, 2 * ST])
        d_eia = nc.dram_tensor("d_eia", [E, P, DT * P], F32, kind="Internal").ap()
        d_eib = nc.dram_tensor("d_eib", [E, 2 * R, F], F32, kind="Internal").ap()
        d_eob = nc.dram_tensor("d_eob", [E, 2 * R, D], F32, kind="Internal").ap()

        hbank = [ctx.enter_context(nc.psum_tensor(f"hbank{n}", [P, 512], F32)) for n in range(2)]
        obank = [ctx.enter_context(nc.psum_tensor(f"obank{n}", [P, 512], F32)) for n in range(3)]
        mbank = [ctx.enter_context(nc.psum_tensor(f"mbank{n}", [P, 512], F32)) for n in range(3)]
        O_OF = (0, 1, 2, 0)
        O_W = (R, 0)
        O_LOW = (0, D)

        WI_BANKS = (obank[2], mbank[0], mbank[1], mbank[2])
        EOA_BANKS = (obank[2], mbank[0])

        names = """ids_in wi_in cia_in ewi_in wo_in coa_in ewo_in w2_in small_in
            x0_in xres_in0 xres_in1 eia_in eib_in eob_in t_in bias_in out_free eia_saved eib_saved eob_saved
            ident_ok ewib_ok ewob_ok masks_ok cnt_ok ones_ok small_ok
            pe_eia pe_eib pe_cib pe_wi pe_cob pe_eob pe_eoa pe_wo pe_w2
            act_eia act_eib act_cib act_wi act_cob act_eob act_eoa act_wo act_w2
            dve_eia dve_eib dve_wi dve_eob dve_eoa dve_wo dve_w2
            pe_h pe_o pe_up pe_lt pe_low pe_x0t pe_x1t pe_tt pe_a pe_sr pe_sc pe_pool pe_x2t
            pe_l2 pe_l3
            act_h act_x0t act_low act_lt act_x1t act_x1h act_tt act_tanh act_th act_srow act_exp
            act_ph act_x2t act_x3h
            dve_h dve_x0t dve_low dve_lowrep dve_lt dve_x1 dve_x1t dve_tt dve_tstk dve_sc dve_max
            dve_arg dve_z dve_x2 dve_x2t dve_x3 dve_out
            pool_x1l pool_eoa pool_pl pool_x2b pool_x3l""".split()
        s = {n: sem(n) for n in names}

        def rows(t, dt_):
            return t.rearrange("(t p) n -> p t n", p=P)

        def sp_stack_in(eng, dst, src, e, reps, signal):
            for r in range(reps):
                eng.dma_start(dst[2 * R * r:2 * R * (r + 1)].bitcast(F32),
                              src[bass.ds(e, 1)].rearrange("e r n -> (e r) n")).then_inc(signal, 16)

        def sp_load(eng, which, i, low, high):
            return [eng.value_load(ids[0:1, which, bass.ds(2 * i + j, 1)], min_val=low, max_val=high)
                    for j in range(2)]

        def sp_eia(eng, es):
            for j, e in enumerate(es):
                eng.dma_start(eia[:, j].rearrange("p k c -> p (k c)").bitcast(F32),
                              d_eia[bass.ds(e, 1)].rearrange("e p n -> (e p) n")).then_inc(s["eia_in"], 16)

        def sp_eib(eng, es):
            for j, e in enumerate(es):
                sp_stack_in(eng, eib[:, j], d_eib, e, 4, s["eib_in"])

        def sp_eob(eng, es):
            for j, e in enumerate(es):
                sp_stack_in(eng, eob[:, j], d_eob, e, 2, s["eob_in"])

        def sp_t(eng, ks):
            for j, k in enumerate(ks):
                eng.dma_start(t_raw[:, j], T[bass.ds(k - 1, 1)].rearrange("e (t p) n -> p (e t) n", p=P)
                              ).then_inc(s["t_in"], 16)

        def sp_bias(eng, es):
            for j, e in enumerate(es):
                eng.dma_start(bias_t[:, j], bias2[bass.ds(e, 1)].to_broadcast([P, D])
                              ).then_inc(s["bias_in"], 16)

        def sp_x(eng, i, dst, j, n, signal):
            eng.dma_start(dst[:, j:j + n].rearrange("p b t d -> p (b t) d"),
                          x[bass.ds(2 * i + j, n)].rearrange("b (t p) d -> p (b t) d", p=P)
                          ).then_inc(signal, 16)

        def sp_body(eng, i, head, tail, nxt):
            if head:
                here = sp_load(eng, 0, i, 0, E - 1)
                steps = sp_load(eng, 2, i, 1, T.shape[0])
            if nxt:
                after = sp_load(eng, 0, i + 1, 0, E - 1)
                eng.wait_ge(s["pe_x0t"], 2 * i + 2)
                sp_x(eng, i + 1, x0, 0, 2, s["x0_in"])
                eng.wait_ge(s["pe_low"], i + 1)
                sp_eia(eng, after)
            if head and tail:
                eng.wait_ge(s["pe_up"], 4 * i)
                sp_eob(eng, here)
                eng.wait_ge(s["pe_tt"], 2 * i)
                sp_t(eng, steps)
            if head and not tail:
                eng.wait_ge(s["pe_w2"], E)
                sp_t(eng, steps)
            if nxt:
                eng.wait_ge(s["pe_h"], FT * (i + 1))
                sp_eib(eng, after)
            if head and tail:
                for j in range(2):
                    eng.wait_ge(s["dve_x2"], 4 * i - 2 + 2 * j)
                    sp_x(eng, i, x1, j, 1, s[f"xres_in{j}"])
                eng.wait_ge(s["pool_x2b"], 2 * i)
                sp_bias(eng, here)
            if tail:
                for j in range(2):
                    eng.wait_ge(s["dve_out"], 2 * i - 1 + j)
                    eng.dma_start(out[bass.ds(2 * (i - 1) + j, 1)].rearrange("b (t p) d -> p (b t) d", p=P),
                                  x2[:, j]).then_inc(s["out_free"], 16)

        def sp_prologue(eng):
            for n, t in enumerate((expert_id, mask_id, step_id)):
                eng.dma_start(ids[0:1, n], t.rearrange("(o n) -> o n", o=1)).then_inc(s["ids_in"], 16)
            eng.dma_start(ewib_raw[:], ewi_b.rearrange("e (p t) r -> p e (t r)", p=P)).then_inc(s["ewi_in"], 16)
            eng.dma_start(ewia_raw[:], ewi_a.rearrange("e r d -> (e r) d")).then_inc(s["ewi_in"], 16)
            eng.dma_start(cib_raw[:], cwi_b.rearrange("(p t) r -> p (t r)", p=P)).then_inc(s["cia_in"], 16)
            eng.dma_start(cia_raw[:], cwi_a).then_inc(s["cia_in"], 16)
            eng.dma_start(wi_raw[:], rows(wi, FT)).then_inc(s["wi_in"], 16)
            sp_x(eng, 0, x0, 0, 2, s["x0_in"])
            eng.dma_start(coa_raw[:], cwo_a).then_inc(s["coa_in"], 16)
            eng.dma_start(cob_raw[:], cwo_b.rearrange("(p t) r -> p (t r)", p=P)).then_inc(s["coa_in"], 16)
            eng.dma_start(ewoa_raw[:], ewo_a.rearrange("e r f -> (e r) f")).then_inc(s["ewo_in"], 16)
            eng.dma_start(ewob_raw[:], ewo_b.rearrange("e (p t) r -> p e (t r)", p=P)).then_inc(s["ewo_in"], 16)
            eng.dma_start(wo_raw[:], rows(wo, DT)).then_inc(s["wo_in"], 16)
            eng.wait_ge(s["ids_in"], 48)
            first = sp_load(eng, 0, 0, 0, E - 1)
            eng.wait_ge(s["dve_eia"], DT)
            eng.dma_start(d_eia.rearrange("e p n -> p e n"),
                          eia_st[:].rearrange("p e k c -> p e (k c)").bitcast(F32)).then_inc(s["eia_saved"], 16)
            eng.wait_ge(s["dve_eib"], 2)
            for hl in range(2):
                eng.dma_start(d_eib[:, hl * R:(hl + 1) * R], eib_st[:, hl].bitcast(F32)).then_inc(s["eib_saved"], 16)
            eng.wait_ge(s["eia_saved"], 16)
            sp_eia(eng, first)
            eng.wait_ge(s["eib_saved"], 32)
            sp_eib(eng, first)
            eng.dma_start(w2_raw[:].rearrange("p e t n -> p (e t) n"),
                          W2.rearrange("e (t p) n -> p (e t) n", p=P)).then_inc(s["w2_in"], 16)
            eng.dma_start(w1_raw[:], W1.rearrange("(t p) a -> p t a", p=P)).then_inc(s["small_in"], 16)
            for n in range(2):
                c = slice(n * A, (n + 1) * A)
                eng.dma_start(b1_c[c], b1.rearrange("(a o) -> a o", o=1)).then_inc(s["small_in"], 16)
                eng.dma_start(v_c[c], v.rearrange("(a o) -> a o", o=1)).then_inc(s["small_in"], 16)
            eng.wait_ge(s["dve_eob"], 1)
            for hl in range(2):
                eng.dma_start(d_eob[:, hl * R:(hl + 1) * R], eob_st[:, hl].bitcast(F32)).then_inc(s["eob_saved"], 16)
            eng.wait_ge(s["eob_saved"], 32)
            sp_eob(eng, first)
            for j in range(2):
                sp_x(eng, 0, x1, j, 1, s[f"xres_in{j}"])
            sp_bias(eng, first)
            eng.sem_inc(s["out_free"], 32)

        def split3(eng, dst, lhs, rhs, first, last):
            (lh, ll), (rh, rl) = lhs, rhs
            eng.matmul(dst, lh, rh, start=first, stop=False, skip_group_check=True)
            eng.matmul(dst, lh, rl, start=False, stop=False, skip_group_check=True)
            return eng.matmul(dst, ll, rh, start=False, stop=last, skip_group_check=True)

        def pe_x0t(eng, i, j):
            for k in range(DT):
                for t in range(ST):
                    at = k * S + t * P
                    m = eng.transpose(hbank[1 - j][:, at:at + P], x0[:, j, t, k * P:(k + 1) * P], ident[:])
            m.then_inc(s["pe_x0t"], 1)

        def pe_low(eng, i):
            eng.wait_ge(s["eia_in"], 32 * (i + 1))
            eng.wait_ge(s["dve_x0t"], 2 * (i + 1))
            for j in range(2):
                c = slice(j * S, (j + 1) * S)
                for k in range(DT):
                    eng.matmul(hbank[1][:, c], eia[:, j, k], x0T_h[:, k, c], start=k == 0 and j == 0,
                               stop=False, skip_group_check=True)
                    m = eng.matmul(hbank[1][:, c], eia[:, j, k], x0T_l[:, k, c], start=False,
                                   stop=k == DT - 1, skip_group_check=True)
            m.then_inc(s["pe_low"], 1)

        def pe_h(eng, i, f):
            if f == 1:
                eng.wait_ge(s["dve_low"], i + 1)
            if f >= 2:
                eng.wait_ge(s["dve_h"], FT * i + f - 1)
            h = hbank[f % 2]
            c = slice(f * P, (f + 1) * P)
            for k in range(DT):
                split3(eng, h[:, :], (wiT_h[:, k, c], wiT_l[:, k, c]), (x0T_h[:, k], x0T_l[:, k]),
                       k == 0, False)
            if f == 0:
                eng.wait_ge(s["eib_in"], 128 * (i + 1))
                eng.wait_ge(s["dve_low"], i + 1)
            for j in range(2):
                q = slice(j * S, (j + 1) * S)
                m = eng.matmul(h[:, q], eib[:, j, c], low[:, q], start=False, stop=j == 1,
                               skip_group_check=True)
            m.then_inc(s["pe_h"], 1)

        def pe_o(eng, i, n):
            j, t = divmod(n, ST)
            if n == 0:
                eng.wait_ge(s["dve_h"], FT * (i + 1))
                eng.wait_ge(s["dve_wo"], FT)
                eng.wait_ge(s["dve_eoa"], 2)
            if n == 0 or n == 2:
                eng.wait_ge(s["pool_eoa"], 4 * i + 2 + n)
            if n == 3:
                eng.wait_ge(s["dve_x1"], 4 * i + 1)
            o = obank[O_OF[n]]
            c0 = j * R
            for f in range(FT):
                q = slice(j * S + t * P, j * S + (t + 1) * P)
                m = split3(eng, o[:, 0:R + D], (hT_h[:, f, q], hT_l[:, f, q]),
                           (woT_h[:, f, c0:c0 + R + D], woT_l[:, f, c0:c0 + R + D]), f == 0, False)
            m.then_inc(s["pe_o"], 1)

        def pe_lt(eng, i, j, nxt):
            eng.wait_ge(s["dve_lowrep"], 4 * i + 2 * j + 2)
            if j and nxt:
                eng.wait_ge(s["dve_x0t"], 2 * (i + 2))
            for t in range(ST):
                m = eng.transpose(hbank[0][:, t * P:(t + 1) * P],
                                  low_o[:, j * ST + t].rearrange("p a r -> p (a r)"), ident[:])
            m.then_inc(s["pe_lt"], 1)

        def pe_up(eng, i, j):
            if j == 0:
                eng.wait_ge(s["eob_in"], 64 * (i + 1))
            eng.wait_ge(s["dve_lt"], 2 * i + j + 1)
            for t in range(ST):
                n = j * ST + t
                w = O_W[j]
                eng.matmul(obank[O_OF[n]][:, w:w + D], lowT[:, n], eob[:, j], start=False, stop=True,
                           skip_group_check=True).then_inc(s["pe_up"], 1)

        def pe_x1t(eng, p, j):
            if j == 0:
                eng.wait_ge(s["dve_x1"], 4 * p + 4)
            for k in range(DT):
                for t in range(ST):
                    at = k * S + t * P
                    m = eng.transpose(mbank[j][:, at:at + P], x1[:, j, t, k * P:(k + 1) * P], ident[:])
            m.then_inc(s["pe_x1t"], 1)

        def pe_tt(eng, p, j):
            if j == 0:
                eng.wait_ge(s["t_in"], 32 * (p + 1))
            bank = mbank[2 - j]
            for k in range(ST):
                for t in range(ST):
                    at = k * S + t * P
                    m = eng.transpose(bank[:, at:at + P], t_raw[:, j, t, k * P:(k + 1) * P], ident[:])
            m.then_inc(s["pe_tt"], 1)

        def pe_a(eng, p):
            eng.wait_ge(s["dve_x1t"], 2 * p + 2)
            for k in range(DT):
                m = split3(eng, mbank[0][:, :], (w1_h[:, k], w1_l[:, k]), (x1T_h[:, k], x1T_l[:, k]),
                           k == 0, k == DT - 1)
            m.then_inc(s["pe_a"], 1)

        def pe_scores(eng, p):
            eng.wait_ge(s["dve_tstk"], p + 1)
            eng.wait_ge(s["dve_tt"], 2 * p + 1)
            eng.matmul(mbank[2][:, :], v_h[:], tstk[:], start=True, stop=False)
            eng.matmul(mbank[2][:, :], v_l[:], tstk[:], start=False, stop=True).then_inc(s["pe_sr"], 1)
            for n in range(2 * ST):
                c = slice(n * P, (n + 1) * P)
                eng.matmul(mbank[0][:, 2 * n:2 * n + 2], tstk[:, c], v_h[:, 0:2], start=True, stop=False)
                m = eng.matmul(mbank[0][:, 2 * n:2 * n + 2], tstk[:, c], v_l[:, 0:2], start=False, stop=True)
            m.then_inc(s["pe_sc"], 1)

        POOL_BANK = (1, 2, 0, 1)

        def pe_pool(eng, p, j):
            if j == 0:
                eng.wait_ge(s["act_x1h"], 2 * p + 2)
                eng.wait_ge(s["pool_x1l"], 2 * p + 2)
                eng.wait_ge(s["dve_tt"], 2 * p + 2)
                eng.wait_ge(s["act_srow"], p + 1)
                eng.wait_ge(s["dve_sc"], p + 1)
            eng.wait_ge(s["pool_pl"], 2 * p + 1 + j)
            for t in range(ST):
                bank = mbank[POOL_BANK[ST * j + t]]
                if j and t:
                    eng.wait_ge(s["dve_x2"], 4 * p + 1)
                c = slice(t * P, (t + 1) * P)
                for l in range(ST):
                    m = split3(eng, bank[:, 0:D + 2], (p_h[:, j, l, c], p_l[:, j, l, c]),
                               (x1_h[:, j, l], x1_l[:, j, l]), l == 0, l == ST - 1)
                m.then_inc(s["pe_pool"], 1)

        def pe_x2t(eng, p, j):
            eng.wait_ge(s["dve_x2"], 4 * p + 2 + 2 * j)
            bank = mbank[2 if j == 0 else 0]
            for k in range(DT):
                for t in range(ST):
                    at = k * S + t * P
                    m = eng.transpose(bank[:, at:at + P], x2[:, j, t, k * P:(k + 1) * P], ident[:])
            m.then_inc(s["pe_x2t"], 1)

        def pe_l2(eng, p, j):
            e = eng.value_load(ids[0:1, 0, bass.ds(2 * p + j, 1)], min_val=0, max_val=E - 1)
            eng.wait_ge(s["dve_x2t"], 2 * p + 1 + j)
            if j == 0:
                eng.wait_ge(s["dve_x2"], 4 * p + 4)
            bank = mbank[1 + j]
            wh = w2T_h[:, bass.ds(e, 1)].rearrange("p e k n -> p (e k) n")
            wl = w2T_l[:, bass.ds(e, 1)].rearrange("p e k n -> p (e k) n")
            for t in range(ST):
                c = slice(j * S + t * P, j * S + (t + 1) * P)
                for k in range(DT):
                    m = split3(eng, bank[:, t * D:(t + 1) * D], (x1T_h[:, k, c], x1T_l[:, k, c]),
                               (wh[:, k], wl[:, k]), k == 0 and t == 0, k == DT - 1)
            m.then_inc(s["pe_l2"], 1)

        def pe_l3(eng, p, j):
            eng.wait_ge(s["pool_x3l"], 2 * p + 1 + j)
            if j == 0:
                eng.wait_ge(s["dve_x2t"], 2 * p + 2)
            bank = mbank[j]
            for t in range(ST):
                for k in range(ST):
                    c = slice(t * P, (t + 1) * P)
                    m = split3(eng, bank[:, t * D:(t + 1) * D], (tT_h[:, j, k, c], tT_l[:, j, k, c]),
                               (x3_h[:, j, k], x3_l[:, j, k]), k == 0 and t == 0, k == ST - 1)
            m.then_inc(s["pe_l3"], 1)

        def pe_w2_prep(eng, e):
            if e == 0:
                eng.wait_ge(s["w2_in"], 16)
                eng.wait_ge(s["dve_wi"], 4)
                eng.wait_ge(s["dve_eoa"], 2)
            if e >= 3:
                eng.wait_ge(s["dve_w2"], e - 2)
            for k in range(DT):
                for t in range(DT):
                    at = k * D + t * P
                    m = eng.transpose(mbank[e % 3][:, at:at + P], w2_raw[:, e, t, k * P:(k + 1) * P], ident[:])
            m.then_inc(s["pe_w2"], 1)

        def pe_body(eng, i, head, tail, nxt):
            p = i - 1
            first = head and not tail
            for f in range(FT):
                if head:
                    pe_h(eng, i, f)
                if first:
                    pe_w2_prep(eng, f)
                if tail and f == 0:
                    pe_x1t(eng, p, 0)
                    pe_x1t(eng, p, 1)
                if tail and f == 1:
                    pe_tt(eng, p, 0)
                if tail and f == 2:
                    pe_a(eng, p)
                if tail and f == 3:
                    pe_tt(eng, p, 1)
                if tail and f == 4:
                    pe_scores(eng, p)
            if head:
                pe_o(eng, i, 0)
            if tail:
                pe_pool(eng, p, 0)
            if head:
                pe_o(eng, i, 1)
            if tail:
                pe_pool(eng, p, 1)
                pe_x2t(eng, p, 0)
            if head:
                pe_lt(eng, i, 0, nxt)
                pe_o(eng, i, 2)
                pe_up(eng, i, 0)
            if tail:
                pe_x2t(eng, p, 1)
                pe_l2(eng, p, 0)
            if nxt:
                eng.wait_ge(s["x0_in"], 16 * (i + 2))
                pe_x0t(eng, i + 1, 0)
                eng.wait_ge(s["dve_lt"], 2 * i + 1)
                pe_x0t(eng, i + 1, 1)
            if head:
                pe_o(eng, i, 3)
            if tail:
                pe_l2(eng, p, 1)
                pe_l3(eng, p, 0)
            if head:
                pe_lt(eng, i, 1, nxt)
            if nxt:
                pe_low(eng, i + 1)
            if tail:
                pe_l3(eng, p, 1)
            if head:
                pe_up(eng, i, 1)

        def pe_prologue(eng):
            eng.wait_ge(s["ids_in"], 48)
            eng.wait_ge(s["ident_ok"], 2)
            eng.wait_ge(s["ewi_in"], 32)
            for k in range(DT):
                m = eng.transpose(mbank[0][:, k * P:(k + 1) * P], ewia_raw[:, k * P:(k + 1) * P], ident[:])
            m.then_inc(s["pe_eia"], 1)
            eng.wait_ge(s["ewib_ok"], 1)
            for t in range(FT):
                m = eng.transpose(mbank[1 + t // 4][:, (t % 4) * P:(t % 4 + 1) * P],
                                  ewib_s[:, t], ident[:])
                if t % 4 == 3:
                    m.then_inc(s["pe_eib"], 1)
            eng.wait_ge(s["cia_in"], 32)
            for t in range(FT):
                m = eng.transpose(obank[t // 4][0:R, (t % 4) * P:(t % 4 + 1) * P],
                                  cib_raw[:, t * R:(t + 1) * R], ident[:])
            m.then_inc(s["pe_cib"], 1)
            eng.wait_ge(s["x0_in"], 16)
            pe_x0t(eng, 0, 0)
            pe_x0t(eng, 0, 1)
            eng.wait_ge(s["wi_in"], 16)
            eng.wait_ge(s["act_cib"], 1)
            for n, bank in enumerate(WI_BANKS):
                k, a = divmod(n, 2)
                if n == 1:
                    eng.wait_ge(s["dve_eia"], DT)
                if n == 2:
                    eng.wait_ge(s["dve_eib"], 2)
                eng.matmul(bank[:, :], cia_raw[:, k * P:(k + 1) * P], cibT[:, a * 512:(a + 1) * 512],
                           start=True, stop=False, skip_group_check=True)
                for t in range(4):
                    m = eng.matmul(bank[:, t * P:(t + 1) * P], wi_raw[:, 4 * a + t, k * P:(k + 1) * P],
                                   ident[:], start=False, stop=True, skip_group_check=True)
                m.then_inc(s["pe_wi"], 1)
            eng.wait_ge(s["coa_in"], 32)
            for t in range(DT):
                m = eng.transpose(obank[0][0:R, t * P:(t + 1) * P], cob_raw[:, t * R:(t + 1) * R], ident[:])
            m.then_inc(s["pe_cob"], 1)
            eng.wait_ge(s["ewo_in"], 32)
            eng.wait_ge(s["ewob_ok"], 1)
            for t in range(DT):
                m = eng.transpose(obank[1][:, t * P:(t + 1) * P], ewob_s[:, t], ident[:])
            m.then_inc(s["pe_eob"], 1)
            for a, bank in enumerate(EOA_BANKS):
                eng.wait_ge(s["dve_wi"], 1 + a)
                for t in range(4):
                    f = 4 * a + t
                    m = eng.transpose(bank[:, t * P:(t + 1) * P], ewoa_raw[:, f * P:(f + 1) * P], ident[:])
                m.then_inc(s["pe_eoa"], 1)
            eng.wait_ge(s["wo_in"], 16)
            eng.wait_ge(s["act_cob"], 1)
            eng.wait_ge(s["dve_eob"], 1)
            for f in range(FT):
                if f >= 2:
                    eng.wait_ge(s["dve_wo"], f - 1)
                o = obank[f % 2]
                eng.matmul(o[:, 0:D], coa_raw[:, f * P:(f + 1) * P], cobT[:], start=True, stop=False,
                           skip_group_check=True)
                for t in range(DT):
                    m = eng.matmul(o[:, t * P:(t + 1) * P], wo_raw[:, t, f * P:(f + 1) * P], ident[:],
                                   start=False, stop=True, skip_group_check=True)
                m.then_inc(s["pe_wo"], 1)
            pe_low(eng, 0)

        def act_x0t(eng, i, j):
            eng.wait_ge(s["pe_x0t"], 2 * i + j + 1)
            nc.scalar.copy(x0T_h[:, :, j * S:(j + 1) * S],
                           hbank[1 - j][:, :].rearrange("p (k n) -> p k n", k=DT)).then_inc(s["act_x0t"], 1)

        def act_body(eng, i, head, tail, nxt):
            p = i - 1
            copy = nc.scalar.copy

            def a_h(f):
                eng.wait_ge(s["pe_h"], FT * i + f + 1)
                nc.scalar.activation(hT_h[:, f], hbank[f % 2][:, :], ACT.Relu).then_inc(s["act_h"], 1)

            def a_lt(j):
                eng.wait_ge(s["pe_lt"], 2 * i + j + 1)
                copy(lowT[:, j * ST:(j + 1) * ST],
                     hbank[0][0:4 * R, 0:S].rearrange("p (t n) -> p t n", t=ST)).then_inc(s["act_lt"], 1)

            def a_exp(j):
                eng.wait_ge(s["dve_arg"], 4 * p + 2 * j + 2)
                nc.scalar.activation(mix[:, j], mix[:, j], ACT.Exp, scale=-1.0).then_inc(s["act_exp"], 1)
                eng.wait_ge(s["act_exp"], 2 * p + j + 1)
                copy(p_h[:, j], mix[:, j]).then_inc(s["act_ph"], 1)

            def a_x3(j):
                eng.wait_ge(s["dve_x3"], 2 * p + j + 1)
                copy(x3_h[:, j], mix[:, j]).then_inc(s["act_x3h"], 1)

            def a_w2(e):
                eng.wait_ge(s["pe_w2"], e + 1)
                copy(w2T_h[:, e], mbank[e % 3][:, :].rearrange("p (k n) -> p k n", k=DT)
                     ).then_inc(s["act_w2"], 1)

            if head and not tail:
                for f in range(FT):
                    a_h(f)
                    a_w2(f)
                head_tiles = ()
            else:
                head_tiles = range(FT) if head else ()
            if 0 in head_tiles:
                a_h(0)
            if tail:
                for j in range(2):
                    eng.wait_ge(s["pe_x1t"], 2 * p + j + 1)
                    copy(x1T_h[:, :, j * S:(j + 1) * S],
                         mbank[j][:, :].rearrange("p (k n) -> p k n", k=DT)).then_inc(s["act_x1t"], 1)
                for j in range(2):
                    copy(x1_h[:, j, :, 0:D], x1[:, j]).then_inc(s["act_x1h"], 1)
            if 1 in head_tiles:
                a_h(1)
            if tail:
                eng.wait_ge(s["pe_tt"], 2 * p + 1)
                copy(tT_h[:, 0], mbank[2][:, :].rearrange("p (k n) -> p k n", k=ST)).then_inc(s["act_tt"], 1)
            if 2 in head_tiles:
                a_h(2)
            if tail:
                eng.wait_ge(s["pe_a"], p + 1)
                nc.scalar.activation(th[:], mbank[0][:, :], ACT.Tanh, bias=b1_c[:]).then_inc(s["act_tanh"], 1)
                eng.wait_ge(s["act_tanh"], p + 1)
                copy(tstk[:], th[:]).then_inc(s["act_th"], 1)
            if 3 in head_tiles:
                a_h(3)
            if tail:
                eng.wait_ge(s["pe_tt"], 2 * p + 2)
                copy(tT_h[:, 1], mbank[1][:, :].rearrange("p (k n) -> p k n", k=ST)).then_inc(s["act_tt"], 1)
            if 4 in head_tiles:
                a_h(4)
            if tail:
                eng.wait_ge(s["pe_sr"], p + 1)
                copy(th[:], mbank[2][:, :]).then_inc(s["act_srow"], 1)
            if 5 in head_tiles:
                a_h(5)
                a_h(6)
            if tail:
                a_exp(0)
            if 7 in head_tiles:
                a_h(7)
            if tail:
                a_exp(1)
                eng.wait_ge(s["pe_x2t"], 2 * p + 1)
                copy(x1T_h[:, :, 0:S],
                     mbank[2][:, :].rearrange("p (k n) -> p k n", k=DT)).then_inc(s["act_x2t"], 1)
            if head:
                a_lt(0)
            if tail:
                eng.wait_ge(s["pe_x2t"], 2 * p + 2)
                copy(x1T_h[:, :, S:N2],
                     mbank[0][:, :].rearrange("p (k n) -> p k n", k=DT)).then_inc(s["act_x2t"], 1)
            if nxt:
                act_x0t(eng, i + 1, 0)
                act_x0t(eng, i + 1, 1)
            if tail:
                a_x3(0)
                a_x3(1)
            if head:
                a_lt(1)
            if nxt:
                eng.wait_ge(s["pe_low"], i + 2)
                copy(low[:], hbank[1][:, :]).then_inc(s["act_low"], 1)

        def act_prologue(eng):
            copy, mul = nc.scalar.copy, nc.scalar.mul
            eng.wait_ge(s["pe_eia"], 1)
            for k in range(DT):
                src = mbank[0][:, k * P:(k + 1) * P].rearrange("p (e o r) -> p e o r", e=E, o=1)
                copy(eia_st[:, :, k, 0:4 * R].rearrange("p e (g r) -> p e g r", g=4),
                     src.to_broadcast([P, E, 4, R])).then_inc(s["act_eia"], 1)
            for a in range(2):
                eng.wait_ge(s["pe_eib"], 1 + a)
                dst = eib_st[:, 0].rearrange("p (n t) -> p t n", t=FT)
                mul(dst[:, 4 * a:4 * a + 4], mbank[1 + a][:, :].rearrange("p (t n) -> p t n", t=4),
                    ALPHA).then_inc(s["act_eib"], 1)
            eng.wait_ge(s["pe_cib"], 1)
            dst = cibT[:].rearrange("r (n t) -> r t n", t=FT)
            for a in range(2):
                m = mul(dst[:, 4 * a:4 * a + 4], obank[a][0:R, :].rearrange("r (t n) -> r t n", t=4), ALPHA)
            m.then_inc(s["act_cib"], 1)
            act_x0t(eng, 0, 0)
            act_x0t(eng, 0, 1)
            for n, bank in enumerate(WI_BANKS):
                k, a = divmod(n, 2)
                eng.wait_ge(s["pe_wi"], 1 + n)
                copy(wiT_h[:, k, a * 512:(a + 1) * 512], bank[:, :]).then_inc(s["act_wi"], 1)
            eng.wait_ge(s["pe_cob"], 1)
            mul(cobT[:].rearrange("r (n t) -> r t n", t=DT),
                obank[0][0:R, 0:D].rearrange("r (t n) -> r t n", t=DT), ALPHA).then_inc(s["act_cob"], 1)
            eng.wait_ge(s["pe_eob"], 1)
            mul(eob_st[:, 0].rearrange("p (n t) -> p t n", t=DT),
                obank[1][:, 0:D].rearrange("p (t n) -> p t n", t=DT), ALPHA).then_inc(s["act_eob"], 1)
            for a, bank in enumerate(EOA_BANKS):
                eng.wait_ge(s["pe_eoa"], 1 + a)
                copy(ewoT_h[:, 4 * a:4 * a + 4], bank[:, :].rearrange("p (t n) -> p t n", t=4)
                     ).then_inc(s["act_eoa"], 1)
            for f in range(FT):
                eng.wait_ge(s["pe_wo"], 1 + f)
                copy(woT_h[:, f, R:R + D], obank[f % 2][:, 0:D]).then_inc(s["act_wo"], 1)
            eng.wait_ge(s["pe_low"], 1)
            copy(low[:], hbank[1][:, :]).then_inc(s["act_low"], 1)
            eng.wait_ge(s["small_in"], 80)

        def minus(dst, src, hi):
            return nc.vector.tensor_tensor(dst, src, hi.bitcast(F32), ALU.subtract)

        def lo_T(lo, hi, bank, j):
            c = slice(j * S, (j + 1) * S)
            return minus(lo[:, :, c], bank[:, :].rearrange("p (k n) -> p k n", k=DT), hi[:, :, c])

        def dve_x0t(eng, i, j):
            eng.wait_ge(s["act_x0t"], 2 * i + j + 1)
            lo_T(x0T_l, x0T_h, hbank[1 - j], j).then_inc(s["dve_x0t"], 1)

        def dve_body(eng, i, head, tail, nxt):
            p = i - 1

            def d_h(f):
                eng.wait_ge(s["act_h"], FT * i + f + 1)
                nc.vector.scalar_tensor_tensor(
                    out=hT_l[:, f], in0=hbank[f % 2][:, :], scalar=0.0, in1=hT_h[:, f].bitcast(F32),
                    op0=ALU.max, op1=ALU.subtract).then_inc(s["dve_h"], 1)

            def d_tt(j):
                eng.wait_ge(s["act_tt"], 2 * p + j + 1)
                minus(tT_l[:, j], mbank[2 - j][:, :].rearrange("p (k n) -> p k n", k=ST),
                      tT_h[:, j]).then_inc(s["dve_tt"], 1)

            def d_lowrep(n):
                j = n // ST
                eng.wait_ge(s["pe_o"], 4 * i + n + 1)
                src = obank[O_OF[n]][:, O_LOW[j]:O_LOW[j] + R].rearrange("p (o r) -> p o r", o=1)
                nc.vector.tensor_copy(low_o[:, n], src.to_broadcast([P, G, R])).then_inc(s["dve_lowrep"], 1)

            def d_lt(j):
                eng.wait_ge(s["act_lt"], 2 * i + j + 1)
                q = slice(2 * R, 4 * R)
                minus(lowT[q, j * ST:(j + 1) * ST], hbank[0][q, 0:S].rearrange("p (t n) -> p t n", t=ST),
                      lowT[q, j * ST:(j + 1) * ST]).then_inc(s["dve_lt"], 1)

            def d_x1(n):
                j, t = divmod(n, ST)
                eng.wait_ge(s["pe_up"], 4 * i + n + 1)
                if t == 0:
                    eng.wait_ge(s[f"xres_in{j}"], 16 * (i + 1))
                nc.vector.tensor_tensor(x1[:, j, t], obank[O_OF[n]][:, O_W[j]:O_W[j] + D], x1[:, j, t],
                                        ALU.add).then_inc(s["dve_x1"], 1)

            def d_pre(j):
                if j == 0:
                    eng.wait_ge(s["act_srow"], p + 1)
                else:
                    eng.wait_ge(s["dve_max"], 6 * p + 3)
                row = th[:, j * S:(j + 1) * S]
                nc.vector.tensor_tensor_scan(pre_max[:, S + 1:], row, row, -BIG, ALU.max,
                                             ALU.max).then_inc(s["dve_max"], 1)

            def d_suf(j):
                row = th[:, (j + 1) * S - 1:j * S - 1:-1] if j else th[:, S - 1::-1]
                nc.vector.tensor_tensor_scan(suf_max[:, S - 1::-1], row, row, -BIG, ALU.max,
                                             ALU.max).then_inc(s["dve_max"], 1)

            def d_rowmax(j):
                kind = eng.value_load(ids[0:1, 1, bass.ds(2 * p + j, 1)], min_val=0, max_val=2)
                a = eng.value_load(pre_at[0:1, bass.ds(kind, 1)], min_val=0, max_val=S + 1)
                b = eng.value_load(suf_at[0:1, bass.ds(kind, 1)], min_val=0, max_val=S + 1)
                eng.wait_ge(s["dve_max"], 6 * p + 3 * j + 2)
                if j:
                    eng.wait_ge(s["dve_arg"], 4 * p + 2)
                nc.vector.tensor_tensor(mrow[:], pre_max[:, bass.ds(a, S)], suf_max[:, bass.ds(b, S)],
                                        ALU.max).then_inc(s["dve_max"], 1)
                return kind

            def d_arg(j, kind):
                eng.wait_ge(s["dve_max"], 6 * p + 3 * j + 3)
                for l in range(ST):
                    mask = mask_big[:, bass.ds(kind, 1), l].rearrange("p o n -> p (o n)")
                    nc.vector.scalar_tensor_tensor(
                        out=mix[:, j, l], in0=mrow[:], scalar=s_col[:, ST * j + l, 0:1], in1=mask,
                        op0=ALU.subtract, op1=ALU.max).then_inc(s["dve_arg"], 1)

            def d_x2(j):
                kind = eng.value_load(ids[0:1, 1, bass.ds(2 * p + j, 1)], min_val=0, max_val=2)
                for t in range(ST):
                    n = ST * j + t
                    bank = mbank[POOL_BANK[n]]
                    eng.wait_ge(s["pe_pool"], 4 * p + n + 1)
                    nc.vector.tensor_tensor(zc[:, n:n + 1], bank[:, D:D + 1], cnt[:, bass.ds(kind, 1), t],
                                            ALU.mult).then_inc(s["dve_z"], 1)
                    eng.wait_ge(s["dve_z"], 8 * p + 2 * n + 1)
                    nc.vector.reciprocal(rz[:, n:n + 1], zc[:, n:n + 1]).then_inc(s["dve_z"], 1)
                    eng.wait_ge(s["dve_z"], 8 * p + 2 * n + 2)
                    if n == 0:
                        eng.wait_ge(s["out_free"], 32 * p + 32)
                    nc.vector.scalar_tensor_tensor(
                        out=x2[:, j, t], in0=bank[:, 0:D], scalar=rz[:, n:n + 1], in1=x1[:, j, t],
                        op0=ALU.mult, op1=ALU.add).then_inc(s["dve_x2"], 1)

            def d_x2t(j):
                eng.wait_ge(s["act_x2t"], 2 * p + j + 1)
                lo_T(x1T_l, x1T_h, mbank[2 if j == 0 else 0], j).then_inc(s["dve_x2t"], 1)

            def d_x3(j):
                eng.wait_ge(s["pe_l2"], 2 * p + j + 1)
                eng.wait_ge(s["pool_x2b"], 2 * p + j + 1)
                nc.vector.tensor_tensor(mix[:, j], mbank[1 + j][:, :].rearrange("p (t n) -> p t n", t=ST),
                                        mix[:, j], ALU.add).then_inc(s["dve_x3"], 1)

            def d_out(j):
                eng.wait_ge(s["pe_l3"], 2 * p + j + 1)
                nc.vector.tensor_tensor(x2[:, j], mbank[j][:, :].rearrange("p (t n) -> p t n", t=ST),
                                        mix[:, j], ALU.add).then_inc(s["dve_out"], 1)

            def d_w2(e):
                eng.wait_ge(s["act_w2"], e + 1)
                minus(w2T_l[:, e], mbank[e % 3][:, :].rearrange("p (k n) -> p k n", k=DT),
                      w2T_h[:, e]).then_inc(s["dve_w2"], 1)

            if head and not tail:
                for f in range(FT):
                    d_h(f)
                    d_w2(f)
                head_tiles = ()
            else:
                head_tiles = range(FT) if head else ()
            if 0 in head_tiles:
                d_h(0)
            if tail:
                for j in range(2):
                    eng.wait_ge(s["act_x1t"], 2 * p + j + 1)
                    lo_T(x1T_l, x1T_h, mbank[j], j).then_inc(s["dve_x1t"], 1)
            if 1 in head_tiles:
                d_h(1)
            if tail:
                d_tt(0)
            if 2 in head_tiles:
                d_h(2)
            if tail:
                eng.wait_ge(s["act_th"], p + 1)
                q = slice(A, P)
                minus(tstk[q], th[q], tstk[q]).then_inc(s["dve_tstk"], 1)
            if 3 in head_tiles:
                d_h(3)
            if tail:
                d_tt(1)
            if 4 in head_tiles:
                d_h(4)
            if tail:
                eng.wait_ge(s["pe_sc"], p + 1)
                nc.vector.tensor_copy(s_col[:], mbank[0][:, 0:4 * ST].rearrange("p (n o) -> p n o", o=2)
                                      ).then_inc(s["dve_sc"], 1)
                d_pre(0)
            if 5 in head_tiles:
                d_h(5)
            if tail:
                d_suf(0)
                kind = d_rowmax(0)
                eng.wait_ge(s["dve_sc"], p + 1)
                d_arg(0, kind)
            if 6 in head_tiles:
                d_h(6)
            if tail:
                d_pre(1)
                d_suf(1)
            if 7 in head_tiles:
                d_h(7)
            if tail:
                kind = d_rowmax(1)
                d_arg(1, kind)
            if head:
                d_lowrep(0)
            if tail:
                d_x2(0)
            if head:
                d_lowrep(1)
            if tail:
                d_x2(1)
                d_x2t(0)
            if head:
                d_lt(0)
                d_lowrep(2)
                d_x1(0)
                d_x1(1)
            if tail:
                d_x2t(1)
                d_x3(0)
            if nxt:
                dve_x0t(eng, i + 1, 0)
                dve_x0t(eng, i + 1, 1)
            if head:
                d_lowrep(3)
            if tail:
                d_x3(1)
                d_out(0)
            if head:
                d_lt(1)
            if nxt:
                dve_low(eng, i + 1)
            if tail:
                d_out(1)
            if head:
                d_x1(2)
                d_x1(3)

        def dve_low(eng, i):
            eng.wait_ge(s["act_low"], i + 1)
            q = slice(32, 64)
            minus(low[q], hbank[1][q, :], low[q])
            q = slice(96, 128)
            minus(low[q], hbank[1][q, :], low[q]).then_inc(s["dve_low"], 1)

        def dve_prologue(eng):
            eng.wait_ge(s["ids_in"], 48)
            eng.wait_ge(s["ewi_in"], 32)
            nc.vector.tensor_copy(ewib_s[:].rearrange("p t (e r) -> p t e r", r=R),
                                  ewib_raw[:].rearrange("p e (t r) -> p t e r", r=R)).then_inc(s["ewib_ok"], 1)
            for k in range(DT):
                eng.wait_ge(s["act_eia"], DT)
                src = mbank[0][:, k * P:(k + 1) * P].rearrange("p (e o r) -> p e o r", e=E, o=1)
                minus(eia_st[:, :, k, 4 * R:].rearrange("p e (g r) -> p e g r", g=4),
                      src.to_broadcast([P, E, 4, R]),
                      eia_st[:, :, k, 0:4 * R].rearrange("p e (g r) -> p e g r", g=4)).then_inc(s["dve_eia"], 1)
            for a in range(2):
                eng.wait_ge(s["act_eib"], 1 + a)
                hi = eib_st[:, 0].rearrange("p (n t) -> p t n", t=FT)[:, 4 * a:4 * a + 4]
                lo = eib_st[:, 1].rearrange("p (n t) -> p t n", t=FT)[:, 4 * a:4 * a + 4]
                nc.vector.scalar_tensor_tensor(
                    out=lo, in0=mbank[1 + a][:, :].rearrange("p (t n) -> p t n", t=4), scalar=ALPHA,
                    in1=hi.bitcast(F32), op0=ALU.mult, op1=ALU.subtract).then_inc(s["dve_eib"], 1)
            dve_x0t(eng, 0, 0)
            dve_x0t(eng, 0, 1)
            for n, bank in enumerate(WI_BANKS):
                k, a = divmod(n, 2)
                eng.wait_ge(s["act_wi"], 1 + n)
                c = slice(a * 512, (a + 1) * 512)
                minus(wiT_l[:, k, c], bank[:, :], wiT_h[:, k, c]).then_inc(s["dve_wi"], 1)
            eng.wait_ge(s["ewo_in"], 32)
            nc.vector.tensor_copy(ewob_s[:].rearrange("p t (e r) -> p t e r", r=R),
                                  ewob_raw[:].rearrange("p e (t r) -> p t e r", r=R)).then_inc(s["ewob_ok"], 1)
            eng.wait_ge(s["act_eob"], 1)
            hi, lo = (eob_st[:, n].rearrange("p (n t) -> p t n", t=DT) for n in range(2))
            nc.vector.scalar_tensor_tensor(
                out=lo, in0=obank[1][:, 0:D].rearrange("p (t n) -> p t n", t=DT), scalar=ALPHA,
                in1=hi.bitcast(F32), op0=ALU.mult, op1=ALU.subtract).then_inc(s["dve_eob"], 1)
            for a, bank in enumerate(EOA_BANKS):
                eng.wait_ge(s["act_eoa"], 1 + a)
                minus(ewoT_l[:, 4 * a:4 * a + 4], bank[:, :].rearrange("p (t n) -> p t n", t=4),
                      ewoT_h[:, 4 * a:4 * a + 4]).then_inc(s["dve_eoa"], 1)
            for f in range(FT):
                eng.wait_ge(s["act_wo"], 1 + f)
                minus(woT_l[:, f, R:R + D], obank[f % 2][:, 0:D], woT_h[:, f, R:R + D]).then_inc(s["dve_wo"], 1)
            dve_low(eng, 0)
            eng.wait_ge(s["small_in"], 80)
            w1 = w1_raw[:].rearrange("p k (o a) -> p k o a", o=1).to_broadcast([P, DT, 2, A])
            w1h, w1l = (t[:].rearrange("p k (o a) -> p k o a", o=2) for t in (w1_h, w1_l))
            nc.vector.tensor_copy(w1h, w1).then_inc(s["small_ok"], 1)
            nc.vector.tensor_copy(v_h[:], v_c[:].to_broadcast([P, P])).then_inc(s["small_ok"], 1)
            eng.wait_ge(s["small_ok"], 2)
            minus(w1l, w1, w1h).then_inc(s["small_ok"], 1)
            minus(v_l[:], v_c[:].to_broadcast([P, P]), v_h[:]).then_inc(s["small_ok"], 1)
            eng.wait_ge(s["masks_ok"], 3)
            eng.wait_ge(s["cnt_ok"], 4)
            nc.vector.tensor_copy(cnt[:], cnt_i[:]).then_inc(s["cnt_ok"], 1)
            eng.wait_ge(s["cnt_ok"], 5)

        def minus_pool(dst, src, hi):
            return nc.gpsimd.tensor_tensor(dst, src, hi.bitcast(F32), ALU.subtract)

        def pool_prologue(eng):
            eng.memset(ident[:], 0.0).then_inc(s["ident_ok"], 1)
            eng.wait_ge(s["ident_ok"], 1)
            eng.affine_select(out=ident[:], in_=ident[:], compare_op=ALU.not_equal, fill=1.0, base=0,
                              pattern=[[-1, P]], channel_multiplier=1).then_inc(s["ident_ok"], 1)
            for k, (a, b) in enumerate(((S + 1, S + 1), (0, 0), (S, 1))):
                eng.memset(pre_at[0:1, k:k + 1], a)
                eng.memset(suf_at[0:1, k:k + 1], b)
            eng.memset(pre_max[:, 0:S + 1], -BIG)
            eng.memset(suf_max[:, S:], -BIG)
            eng.memset(mask_big[:], 0.0).then_inc(s["masks_ok"], 1)
            eng.iota(cnt_i[:, 0], pattern=[[P, ST]], base=1, channel_multiplier=1).then_inc(s["cnt_ok"], 1)
            eng.iota(cnt_i[:, 1], pattern=[[-P, ST]], base=S, channel_multiplier=-1).then_inc(s["cnt_ok"], 1)
            eng.iota(cnt_i[:, 2], pattern=[[0, ST]], base=S - 1, channel_multiplier=0).then_inc(s["cnt_ok"], 1)
            eng.wait_ge(s["masks_ok"], 1)
            for k, (sign, op) in enumerate(((1, ALU.is_ge), (-1, ALU.is_ge), (1, ALU.not_equal))):
                m = eng.affine_select(out=mask_big[:, k], in_=mask_big[:, k], compare_op=op, fill=BIG, base=0,
                                      pattern=[[-sign * P, ST], [sign, S]], channel_multiplier=-sign)
            m.then_inc(s["masks_ok"], 2)
            eng.memset(s_col[:, 0, 0:1], 0.0).then_inc(s["cnt_ok"], 1)
            eng.wait_ge(s["ids_in"], 48)

        def pool_body(eng, i, head, tail, nxt):
            p = i - 1
            if head and not tail:
                eng.wait_ge(s["dve_eoa"], 2)
            if tail:
                eng.wait_ge(s["dve_x1"], 4 * p + 4)
                for j in range(2):
                    eng.wait_ge(s["act_x1h"], 2 * p + j + 1)
                    minus_pool(x1_l[:, j, :, 0:D], x1[:, j], x1_h[:, j, :, 0:D]).then_inc(s["pool_x1l"], 1)
            if head:
                for j in range(2):
                    e = eng.value_load(ids[0:1, 0, bass.ds(2 * i + j, 1)], min_val=0, max_val=E - 1)
                    if j == 0 and tail:
                        eng.wait_ge(s["pe_o"], 4 * i)
                    c = slice(j * (R + D), j * (R + D) + R)
                    for src, dst in ((ewoT_h, woT_h), (ewoT_l, woT_l)):
                        nc.gpsimd.tensor_copy(dst[:, :, c], src[:, :, bass.ds(e * R, R)].bitcast(F32)
                                              ).then_inc(s["pool_eoa"], 1)
            if head and not tail:
                eng.wait_ge(s["pe_w2"], E)
                eng.memset(x1_h[:, :, :, D:].bitcast(F32), 1.0).then_inc(s["ones_ok"], 1)
                eng.memset(x1_l[:, :, :, D:].bitcast(F32), 0.0).then_inc(s["ones_ok"], 1)
            if tail:
                for j in range(2):
                    eng.wait_ge(s["act_ph"], 2 * p + j + 1)
                    minus_pool(p_l[:, j], mix[:, j], p_h[:, j]).then_inc(s["pool_pl"], 1)
                eng.wait_ge(s["bias_in"], 32 * (p + 1))
                for j in range(2):
                    eng.wait_ge(s["dve_x2"], 4 * p + 2 * j + 2)
                    b = bias_t[:, j:j + 1].to_broadcast([P, ST, D])
                    nc.gpsimd.tensor_tensor(mix[:, j], x2[:, j], b, ALU.add).then_inc(s["pool_x2b"], 1)
                for j in range(2):
                    eng.wait_ge(s["act_x3h"], 2 * p + j + 1)
                    minus_pool(x3_l[:, j], mix[:, j], x3_h[:, j]).then_inc(s["pool_x3l"], 1)

        def run(eng, prologue, body):
            prologue(eng)
            body(eng, 0, True, False, True)
            with eng.Fori(1, PAIRS - 1) as i:
                body(eng, i, True, True, True)
            body(eng, PAIRS - 1, True, True, False)
            body(eng, PAIRS, False, True, False)

        block = ctx.enter_context(nc.Block())

        @block.sync
        def _(eng):
            run(eng, sp_prologue, sp_body)
            eng.wait_ge(s["out_free"], 32 * PAIRS + 32)

        @block.tensor
        def _(eng):
            run(eng, pe_prologue, pe_body)

        @block.scalar
        def _(eng):
            run(eng, act_prologue, act_body)

        @block.vector
        def _(eng):
            run(eng, dve_prologue, dve_body)

        @block.gpsimd
        def _(eng):
            run(eng, pool_prologue, pool_body)


_INS = ['x', 'itok_B_0_7', 'itok_B_0_2', 'itok_B_1_98', 'L0_cond_wi', 'L0_cond_wo', 'L0_cond_common_wi_a',
        'L0_cond_common_wi_b', 'L0_cond_common_wo_a', 'L0_cond_common_wo_b', 'L0_cond_experts_wi_a',
        'L0_cond_experts_wi_b', 'L0_cond_experts_wo_a', 'L0_cond_experts_wo_b', 'L1_cond_W1', 'L1_cond_b1',
        'L1_cond_v', 'L2_cond_weight', 'L2_cond_bias', 'L3_cond_T']


def kernel(**inputs):
    import numpy as _np
    import concourse.bacc as _bacc
    from concourse import mybir as _mybir
    from concourse.bass_utils import run_bass_kernel_spmd as _run

    nc = _bacc.Bacc("TRN2", target_bir_lowering=False, num_devices=1)
    arrays, args = {}, []
    for name in _INS:
        a = _np.ascontiguousarray(inputs[name])
        arrays[f"in_{name}_dram"] = a
        args.append(nc.dram_tensor(f"in_{name}_dram", a.shape, _mybir.dt.from_np(a.dtype), kind="ExternalInput").ap())
    shape = arrays["in_x_dram"].shape
    args.append(nc.dram_tensor("out_0_dram", shape, _mybir.dt.from_np(_np.dtype("float32")), kind="ExternalOutput").ap())
    build(nc, *args)
    r = _run(nc, [arrays], core_ids=[0])
    return r.results[0]["out_0_dram"]
```

```python
from contextlib import ExitStack

import concourse.bass as bass
from concourse import mybir

F32 = mybir.dt.float32
F32R = mybir.dt.float32r
BF16 = mybir.dt.bfloat16
I32 = mybir.dt.int32
ALU = mybir.AluOpType
AX = mybir.AxisListType
ACT = mybir.ActivationFunctionType

P = 128
BIG = 1.0e30
ALPHA = 2.0


def build(nc, x, expert_id, mask_id, step_id, wi, wo, cwi_a, cwi_b, cwo_a, cwo_b,
          ewi_a, ewi_b, ewo_a, ewo_b, W1, b1, v, W2, bias2, T, out):
    B, S, D = x.shape
    F = wi.shape[0]
    E, R, _ = ewi_a.shape
    A = W1.shape[1]
    ST, DT, FT = S // P, D // P, F // P
    PAIRS = B // 2
    N2 = 2 * S
    G = P // R
    assert (ST, DT, 2 * A, E * R, G) == (2, 2, P, P, 8)

    with ExitStack() as ctx:
        def sb(name, shape, dt=F32):
            return ctx.enter_context(nc.sbuf_tensor(name, shape, dt))

        def sem(name):
            return ctx.enter_context(nc.semaphore(name))

        ids = sb("ids", [1, 3, B], I32)
        ident = sb("ident", [P, P])
        wiT_h = sb("wiT_h", [P, DT, F], F32R)
        wiT_l = sb("wiT_l", [P, DT, F], F32R)
        woT_h = sb("woT_h", [P, FT, R + D + R], F32R)
        woT_l = sb("woT_l", [P, FT, R + D + R], F32R)
        ewoT_h = sb("ewoT_h", [P, FT, E * R], F32R)
        ewoT_l = sb("ewoT_l", [P, FT, E * R], F32R)
        w2T_h = sb("w2T_h", [P, E, DT, D], F32R)
        w2T_l = sb("w2T_l", [P, E, DT, D], F32R)
        w1_h = sb("w1_h", [P, DT, P], F32R)
        w1_l = sb("w1_l", [P, DT, P], F32R)
        v_h = sb("v_h", [P, P], F32R)
        v_l = sb("v_l", [P, P], F32R)
        b1_c = sb("b1_c", [P, 1])
        v_c = sb("v_c", [P, 1])
        mask_big = sb("mask_big", [P, 3, ST, S], BF16)
        cnt = sb("cnt", [P, 3, ST])
        cnt_i = sb("cnt_i", [P, 3, ST], I32)
        pre_at = sb("pre_at", [1, 3], I32)
        suf_at = sb("suf_at", [1, 3], I32)
        pre_max = sb("pre_max", [P, S + 1 + S])
        suf_max = sb("suf_max", [P, S + S + 1])

        raw = ExitStack()

        def rb(name, shape, dt=F32):
            return raw.enter_context(nc.sbuf_tensor(name, shape, dt))

        w2_raw = rb("w2_raw", [P, E, DT, D])
        wo_raw = rb("wo_raw", [P, DT, F])
        coa_raw = rb("coa_raw", [R, F])
        cob_raw = rb("cob_raw", [P, DT * R])
        cobT = rb("cobT", [R, D])
        ewoa_raw = rb("ewoa_raw", [P, F])
        ewob_raw = rb("ewob_raw", [P, E, DT * R])
        ewob_s = rb("ewob_s", [P, DT, E * R])
        w1_raw = rb("w1_raw", [P, DT, A])
        eob_st = rb("eob_st", [P, 2, D], F32R)
        eia_st = rb("eia_st", [P, E, DT, P], F32R)
        rb("fill", [P, 704])
        wi_raw = rb("wi_raw", [P, FT, D])
        cia_raw = rb("cia_raw", [R, D])
        cib_raw = rb("cib_raw", [P, FT * R])
        cibT = rb("cibT", [R, F])
        ewia_raw = rb("ewia_raw", [P, D])
        ewib_raw = rb("ewib_raw", [P, E, FT * R])
        ewib_s = rb("ewib_s", [P, FT, E * R])
        eib_st = rb("eib_st", [P, 2, F], F32R)
        raw.close()

        x1T_h = sb("x1T_h", [P, DT, N2], F32R)
        x1T_l = sb("x1T_l", [P, DT, N2], F32R)
        th = sb("th", [P, N2])
        tstk = sb("tstk", [P, N2], F32R)
        terms = sb("terms", [P, 2, ST, S])
        p_h = sb("p_h", [P, 2, ST, S], F32R)
        p_l = sb("p_l", [P, 2, ST, S], F32R)
        x1_h = sb("x1_h", [P, 2, ST, D + 2], F32R)
        x1_l = sb("x1_l", [P, 2, ST, D + 2], F32R)
        x2 = sb("x2", [P, 2, ST, D])
        t_raw = sb("t_raw", [P, 2, ST, S])
        tT_h = sb("tT_h", [P, 2, ST, S], F32R)
        tT_l = sb("tT_l", [P, 2, ST, S], F32R)
        hT_h = sb("hT_h", [P, FT, N2], F32R)
        hT_l = sb("hT_l", [P, FT, N2], F32R)
        x2_h, x2_l = p_h, p_l
        x0 = sb("x0", [P, 2, ST, D])
        x0T_h = sb("x0T_h", [P, DT, N2], F32R)
        x0T_l = sb("x0T_l", [P, DT, N2], F32R)
        eia = sb("eia", [P, 2, DT, P], F32R)
        eib = sb("eib", [P, 2, F], F32R)
        low = sb("low", [P, N2], F32R)
        eob = sb("eob", [4 * R, 2, D], F32R)
        low_o = sb("low_o", [P, 2 * ST, G, R])
        lowT = sb("lowT", [4 * R, 2 * ST, P], F32R)
        x1 = sb("x1", [P, 2, ST, D])
        bias_t = sb("bias_t", [P, 2, D])
        mrow = sb("mrow", [P, S])
        s_col = sb("s_col", [P, 2 * ST])
        rowsum = sb("rowsum", [P, 2 * ST])
        zc = sb("zc", [P, 2 * ST])
        rz = sb("rz", [P, 2 * ST])
        d_eia = nc.dram_tensor("d_eia", [E, P, DT * P], F32, kind="Internal").ap()
        d_eib = nc.dram_tensor("d_eib", [E, 2 * R, F], F32, kind="Internal").ap()
        d_eob = nc.dram_tensor("d_eob", [E, 2 * R, D], F32, kind="Internal").ap()

        hbank = [ctx.enter_context(nc.psum_tensor(f"hbank{n}", [P, 512], F32)) for n in range(2)]
        obank = [ctx.enter_context(nc.psum_tensor(f"obank{n}", [P, 512], F32)) for n in range(3)]
        mbank = [ctx.enter_context(nc.psum_tensor(f"mbank{n}", [P, 512], F32)) for n in range(3)]
        H_BANKS = (hbank[0], hbank[1], obank[1], obank[2])
        O_OF = (0, 1, 2, 0)
        O_W = (R, 0)
        O_LOW = (0, D)

        WI_BANKS = (obank[2], mbank[0], mbank[1], mbank[2])
        EOA_BANKS = (obank[2], mbank[0])

        names = """ids_in wi_in cia_in ewi_in wo_in coa_in ewo_in w2_in small_in
            x0_in xres_in0 xres_in1 eia_in eib_in eob_in t_in bias_in out_free eia_saved eib_saved eob_saved
            ident_ok ewib_ok ewob_ok masks_ok cnt_ok ones_ok small_ok
            pe_eia pe_eib pe_cib pe_wi pe_cob pe_eob pe_eoa pe_wo pe_w2
            act_eia act_eib act_cib act_wi act_cob act_eob act_eoa act_wo act_w2
            dve_eia dve_eib dve_wi dve_eob dve_eoa dve_wo dve_w2
            pe_h pe_o pe_up pe_lt pe_low pe_x0t pe_x1t pe_tt pe_a pe_sr pe_pool pe_ut
            pe_out
            act_h act_x0t act_low act_lt act_x1t act_x1h act_tt act_tanh act_th act_srow act_exp
            act_ph act_x2h act_ut
            dve_h dve_x0t dve_low dve_lowrep dve_lt dve_x1 dve_x1t dve_tt dve_tstk dve_sc dve_max
            dve_arg dve_z dve_x2 dve_rs dve_ut dve_out
            pool_ti pool_x1l pool_eoa pool_pl pool_x2l w2_ok""".split()
        s = {n: sem(n) for n in names}

        def rows(t, dt_):
            return t.rearrange("(t p) n -> p t n", p=P)

        def sp_stack_in(eng, dst, src, e, reps, signal):
            for r in range(reps):
                eng.dma_start(dst[2 * R * r:2 * R * (r + 1)].bitcast(F32),
                              src[bass.ds(e, 1)].rearrange("e r n -> (e r) n")).then_inc(signal, 16)

        def sp_load(eng, which, i, low, high):
            return [eng.value_load(ids[0:1, which, bass.ds(2 * i + j, 1)], min_val=low, max_val=high)
                    for j in range(2)]

        def sp_eia(eng, es):
            for j, e in enumerate(es):
                eng.dma_start(eia[:, j].rearrange("p k c -> p (k c)").bitcast(F32),
                              d_eia[bass.ds(e, 1)].rearrange("e p n -> (e p) n")).then_inc(s["eia_in"], 16)

        def sp_eib(eng, es):
            for j, e in enumerate(es):
                sp_stack_in(eng, eib[:, j], d_eib, e, 4, s["eib_in"])

        def sp_eob(eng, es):
            for j, e in enumerate(es):
                sp_stack_in(eng, eob[:, j], d_eob, e, 2, s["eob_in"])

        def sp_t(eng, ks):
            for j, k in enumerate(ks):
                eng.dma_start(t_raw[:, j], T[bass.ds(k - 1, 1)].rearrange("e (t p) n -> p (e t) n", p=P)
                              ).then_inc(s["t_in"], 16)

        def sp_bias(eng, es):
            for j, e in enumerate(es):
                eng.dma_start(bias_t[:, j], bias2[bass.ds(e, 1)].to_broadcast([P, D])
                              ).then_inc(s["bias_in"], 16)

        def sp_x(eng, i, dst, j, n, signal):
            eng.dma_start(dst[:, j:j + n].rearrange("p b t d -> p (b t) d"),
                          x[bass.ds(2 * i + j, n)].rearrange("b (t p) d -> p (b t) d", p=P)
                          ).then_inc(signal, 16)

        def sp_body(eng, i, head, tail, nxt):
            if head:
                here = sp_load(eng, 0, i, 0, E - 1)
                steps = sp_load(eng, 2, i, 1, T.shape[0])
            if nxt:
                after = sp_load(eng, 0, i + 1, 0, E - 1)
                eng.wait_ge(s["pe_x0t"], 2 * i + 2)
                sp_x(eng, i + 1, x0, 0, 2, s["x0_in"])
                eng.wait_ge(s["pe_low"], i + 1)
                sp_eia(eng, after)
            if head and tail:
                eng.wait_ge(s["pe_up"], 4 * i)
                sp_eob(eng, here)
                eng.wait_ge(s["pe_tt"], 2 * i)
                eng.wait_ge(s["dve_rs"], 2 * i)
                sp_t(eng, steps)
            if head and not tail:
                eng.wait_ge(s["pe_w2"], E)
                sp_t(eng, steps)
            if nxt:
                eng.wait_ge(s["pe_h"], FT * (i + 1))
                sp_eib(eng, after)
            if head and tail:
                for j in range(2):
                    eng.wait_ge(s["dve_x2"], 4 * i - 2 + 2 * j)
                    sp_x(eng, i, x1, j, 1, s[f"xres_in{j}"])
            if tail:
                for j in range(2):
                    eng.wait_ge(s["dve_out"], 2 * i + j)
                    eng.dma_start(out[bass.ds(2 * (i - 1) + j, 1)].rearrange("b (t p) d -> p (b t) d", p=P),
                                  x2[:, j]).then_inc(s["out_free"], 16)
            if head and tail:
                sp_bias(eng, here)

        def sp_prologue(eng):
            for n, t in enumerate((expert_id, mask_id, step_id)):
                eng.dma_start(ids[0:1, n], t.rearrange("(o n) -> o n", o=1)).then_inc(s["ids_in"], 16)
            eng.dma_start(ewib_raw[:], ewi_b.rearrange("e (p t) r -> p e (t r)", p=P)).then_inc(s["ewi_in"], 16)
            eng.dma_start(ewia_raw[:], ewi_a.rearrange("e r d -> (e r) d")).then_inc(s["ewi_in"], 16)
            eng.dma_start(cib_raw[:], cwi_b.rearrange("(p t) r -> p (t r)", p=P)).then_inc(s["cia_in"], 16)
            eng.dma_start(cia_raw[:], cwi_a).then_inc(s["cia_in"], 16)
            eng.dma_start(wi_raw[:], rows(wi, FT)).then_inc(s["wi_in"], 16)
            sp_x(eng, 0, x0, 0, 2, s["x0_in"])
            eng.dma_start(coa_raw[:], cwo_a).then_inc(s["coa_in"], 16)
            eng.dma_start(cob_raw[:], cwo_b.rearrange("(p t) r -> p (t r)", p=P)).then_inc(s["coa_in"], 16)
            eng.dma_start(ewoa_raw[:], ewo_a.rearrange("e r f -> (e r) f")).then_inc(s["ewo_in"], 16)
            eng.dma_start(ewob_raw[:], ewo_b.rearrange("e (p t) r -> p e (t r)", p=P)).then_inc(s["ewo_in"], 16)
            eng.dma_start(wo_raw[:], rows(wo, DT)).then_inc(s["wo_in"], 16)
            eng.wait_ge(s["ids_in"], 48)
            first = sp_load(eng, 0, 0, 0, E - 1)
            eng.wait_ge(s["dve_eia"], DT)
            eng.dma_start(d_eia.rearrange("e p n -> p e n"),
                          eia_st[:].rearrange("p e k c -> p e (k c)").bitcast(F32)).then_inc(s["eia_saved"], 16)
            eng.wait_ge(s["dve_eib"], 2)
            for hl in range(2):
                eng.dma_start(d_eib[:, hl * R:(hl + 1) * R], eib_st[:, hl].bitcast(F32)).then_inc(s["eib_saved"], 16)
            eng.wait_ge(s["eia_saved"], 16)
            sp_eia(eng, first)
            eng.wait_ge(s["eib_saved"], 32)
            sp_eib(eng, first)
            eng.dma_start(w2_raw[:].rearrange("p e t n -> p (e t) n"),
                          W2.rearrange("e (t p) n -> p (e t) n", p=P)).then_inc(s["w2_in"], 16)
            eng.dma_start(w1_raw[:], W1.rearrange("(t p) a -> p t a", p=P)).then_inc(s["small_in"], 16)
            for n in range(2):
                c = slice(n * A, (n + 1) * A)
                eng.dma_start(b1_c[c], b1.rearrange("(a o) -> a o", o=1)).then_inc(s["small_in"], 16)
                eng.dma_start(v_c[c], v.rearrange("(a o) -> a o", o=1)).then_inc(s["small_in"], 16)
            eng.wait_ge(s["dve_eob"], 1)
            for hl in range(2):
                eng.dma_start(d_eob[:, hl * R:(hl + 1) * R], eob_st[:, hl].bitcast(F32)).then_inc(s["eob_saved"], 16)
            eng.wait_ge(s["eob_saved"], 32)
            sp_eob(eng, first)
            for j in range(2):
                sp_x(eng, 0, x1, j, 1, s[f"xres_in{j}"])
            sp_bias(eng, first)
            eng.sem_inc(s["out_free"], 32)

        def split3(eng, dst, lhs, rhs, first, last):
            (lh, ll), (rh, rl) = lhs, rhs
            eng.matmul(dst, lh, rh, start=first, stop=False, skip_group_check=True)
            eng.matmul(dst, lh, rl, start=False, stop=False, skip_group_check=True)
            return eng.matmul(dst, ll, rh, start=False, stop=last, skip_group_check=True)

        def pe_x0t(eng, i, j):
            for k in range(DT):
                for t in range(ST):
                    at = k * S + t * P
                    m = eng.transpose(hbank[1 - j][:, at:at + P], x0[:, j, t, k * P:(k + 1) * P], ident[:])
            m.then_inc(s["pe_x0t"], 1)

        def pe_low(eng, i):
            eng.wait_ge(s["eia_in"], 32 * (i + 1))
            eng.wait_ge(s["dve_x0t"], 2 * (i + 1))
            for j in range(2):
                c = slice(j * S, (j + 1) * S)
                for k in range(DT):
                    eng.matmul(hbank[1][:, c], eia[:, j, k], x0T_h[:, k, c], start=k == 0 and j == 0,
                               stop=False, skip_group_check=True)
                    m = eng.matmul(hbank[1][:, c], eia[:, j, k], x0T_l[:, k, c], start=False,
                                   stop=k == DT - 1, skip_group_check=True)
            m.then_inc(s["pe_low"], 1)

        def pe_h(eng, i, f, tail):
            if f == 1:
                eng.wait_ge(s["dve_low"], i + 1)
            if f == 2:
                eng.wait_ge(s["dve_wo"], FT)
                eng.wait_ge(s["dve_eoa"], 2)
            if f >= 4:
                eng.wait_ge(s["dve_h"], FT * i + f - 3)
            h = H_BANKS[f % 4]
            c = slice(f * P, (f + 1) * P)
            for k in range(DT):
                split3(eng, h[:, :], (wiT_h[:, k, c], wiT_l[:, k, c]), (x0T_h[:, k], x0T_l[:, k]),
                       k == 0, False)
            if f == 0:
                if tail:
                    pe_x1t(eng, i - 1, 0)
                eng.wait_ge(s["eib_in"], 128 * (i + 1))
                eng.wait_ge(s["dve_low"], i + 1)
            for j in range(2):
                q = slice(j * S, (j + 1) * S)
                m = eng.matmul(h[:, q], eib[:, j, c], low[:, q], start=False, stop=j == 1,
                               skip_group_check=True)
            m.then_inc(s["pe_h"], 1)

        def pe_o(eng, i, n):
            j, t = divmod(n, ST)
            if n in (0, 2):
                eng.wait_ge(s["pool_eoa"], 4 * i + 2 + n)
            if n == 3:
                eng.wait_ge(s["dve_x1"], 4 * i + 1)
            o = obank[O_OF[n]]
            c0 = j * R
            for f in range(FT):
                if n == 0 and f in (0, FT - 2, FT - 1):
                    eng.wait_ge(s["dve_h"], FT * i + max(f + 1, FT - 2))
                q = slice(j * S + t * P, j * S + (t + 1) * P)
                m = split3(eng, o[:, 0:R + D], (hT_h[:, f, q], hT_l[:, f, q]),
                           (woT_h[:, f, c0:c0 + R + D], woT_l[:, f, c0:c0 + R + D]), f == 0, False)
            m.then_inc(s["pe_o"], 1)

        def pe_lt(eng, i, j, nxt):
            eng.wait_ge(s["dve_lowrep"], 4 * i + 2 * j + 2)
            if j and nxt:
                eng.wait_ge(s["dve_x0t"], 2 * (i + 2))
            for t in range(ST):
                m = eng.transpose(hbank[0][:, t * P:(t + 1) * P],
                                  low_o[:, j * ST + t].rearrange("p a r -> p (a r)"), ident[:])
            m.then_inc(s["pe_lt"], 1)

        def pe_up(eng, i, j):
            if j == 0:
                eng.wait_ge(s["eob_in"], 64 * (i + 1))
            eng.wait_ge(s["dve_lt"], 2 * i + j + 1)
            for t in range(ST):
                n = j * ST + t
                w = O_W[j]
                eng.matmul(obank[O_OF[n]][:, w:w + D], lowT[:, n], eob[:, j], start=False, stop=True,
                           skip_group_check=True).then_inc(s["pe_up"], 1)

        def pe_x1t(eng, p, j):
            if j == 0:
                eng.wait_ge(s["dve_x1"], 4 * p + 4)
            for k in range(DT):
                for t in range(ST):
                    at = k * S + t * P
                    m = eng.transpose(mbank[j][:, at:at + P], x1[:, j, t, k * P:(k + 1) * P], ident[:])
            m.then_inc(s["pe_x1t"], 1)

        def pe_tt(eng, p, j):
            if j == 0:
                eng.wait_ge(s["pool_ti"], 4 * p + 4)
                eng.wait_ge(s["dve_out"], 2 * p + 1)
            bank = mbank[2 - j]
            for k in range(ST):
                for t in range(ST):
                    at = k * S + t * P
                    m = eng.transpose(bank[:, at:at + P], t_raw[:, j, t, k * P:(k + 1) * P], ident[:])
            m.then_inc(s["pe_tt"], 1)

        def pe_a(eng, p):
            eng.wait_ge(s["dve_x1t"], 2 * p + 2)
            for k in range(DT):
                m = split3(eng, mbank[0][:, :], (w1_h[:, k], w1_l[:, k]), (x1T_h[:, k], x1T_l[:, k]),
                           k == 0, k == DT - 1)
            m.then_inc(s["pe_a"], 1)

        def pe_scores(eng, p):
            eng.wait_ge(s["dve_tstk"], p + 1)
            eng.wait_ge(s["dve_tt"], 2 * p + 1)
            eng.matmul(mbank[2][:, :], v_h[:], tstk[:], start=True, stop=False)
            eng.matmul(mbank[2][:, :], v_l[:], tstk[:], start=False, stop=True).then_inc(s["pe_sr"], 1)

        POOL_BANK = (1, 2, 0, 1)

        def pe_pool(eng, p, j):
            if j == 0:
                eng.wait_ge(s["act_x1h"], 2 * p + 2)
                eng.wait_ge(s["pool_x1l"], 2 * p + 2)
                eng.wait_ge(s["dve_tt"], 2 * p + 2)
                eng.wait_ge(s["act_srow"], p + 1)
            eng.wait_ge(s["pool_pl"], 2 * p + 1 + j)
            for t in range(ST):
                bank = mbank[POOL_BANK[ST * j + t]]
                if j and t:
                    eng.wait_ge(s["dve_x2"], 4 * p + 1)
                c = slice(t * P, (t + 1) * P)
                for l in range(ST):
                    m = split3(eng, bank[:, 0:D + 2], (p_h[:, j, l, c], p_l[:, j, l, c]),
                               (x1_h[:, j, l], x1_l[:, j, l]), l == 0, l == ST - 1)
                m.then_inc(s["pe_pool"], 1)

        UT_BANK = (2, 0)

        def pe_ut(eng, p, j):
            eng.wait_ge(s["pool_x2l"], 2 * p + 1 + j)
            eng.wait_ge(s["dve_tt"], 2 * p + 2)
            bank = mbank[UT_BANK[j]]
            for d in range(DT):
                c = slice(d * P, (d + 1) * P)
                for k in range(ST):
                    m = split3(eng, bank[:, d * S:(d + 1) * S], (x2_h[:, j, k, c], x2_l[:, j, k, c]),
                               (tT_h[:, j, k], tT_l[:, j, k]), k == 0 and d == 0, k == ST - 1)
            m.then_inc(s["pe_ut"], 1)

        def pe_expert(eng, p, j):
            return eng.value_load(ids[0:1, 0, bass.ds(2 * p + j, 1)], min_val=0, max_val=E - 1)

        def pe_out(eng, p, j, t, e):
            if t == 0:
                eng.wait_ge(s["dve_ut"], 2 * p + 1 + j)
            if j == 0 and t == 0:
                eng.wait_ge(s["dve_x2"], 4 * p + 4)
            bank = mbank[1 + j]
            wh = w2T_h[:, bass.ds(e, 1)].rearrange("p e k n -> p (e k) n")
            wl = w2T_l[:, bass.ds(e, 1)].rearrange("p e k n -> p (e k) n")
            c = slice(j * S + t * P, j * S + (t + 1) * P)
            for k in range(DT):
                m = split3(eng, bank[:, t * D:(t + 1) * D], (x1T_h[:, k, c], x1T_l[:, k, c]),
                           (wh[:, k], wl[:, k]), k == 0 and t == 0, k == DT - 1)
            m.then_inc(s["pe_out"], 1)

        def pe_w2_prep(eng, e):
            if e == 0:
                eng.wait_ge(s["w2_ok"], 2)
                eng.wait_ge(s["dve_wi"], 4)
                eng.wait_ge(s["dve_eoa"], 2)
            if e >= 3:
                eng.wait_ge(s["dve_w2"], e - 2)
            for k in range(DT):
                for t in range(DT):
                    at = k * D + t * P
                    m = eng.transpose(mbank[e % 3][:, at:at + P], w2_raw[:, e, t, k * P:(k + 1) * P], ident[:])
            m.then_inc(s["pe_w2"], 1)

        def pe_body(eng, i, head, tail, nxt):
            p = i - 1
            first = head and not tail
            for f in range(FT):
                if head:
                    pe_h(eng, i, f, tail)
                if first:
                    pe_w2_prep(eng, f)
                if tail and f == 0:
                    if not head:
                        pe_x1t(eng, p, 0)
                    pe_x1t(eng, p, 1)
                if tail and f == 1:
                    pe_tt(eng, p, 0)
                    pe_a(eng, p)
                if tail and f == 2:
                    pe_tt(eng, p, 1)
                if tail and f == 3:
                    pe_scores(eng, p)
            if head:
                pe_o(eng, i, 0)
            if tail:
                pe_pool(eng, p, 0)
            if head:
                pe_o(eng, i, 1)
            if tail:
                pe_pool(eng, p, 1)
                pe_ut(eng, p, 0)
            if head:
                pe_lt(eng, i, 0, nxt)
                pe_o(eng, i, 2)
                pe_up(eng, i, 0)
            if tail:
                pe_ut(eng, p, 1)
                e0 = pe_expert(eng, p, 0)
                pe_out(eng, p, 0, 0, e0)
                pe_out(eng, p, 0, 1, e0)
            if nxt:
                eng.wait_ge(s["x0_in"], 16 * (i + 2))
                pe_x0t(eng, i + 1, 0)
                eng.wait_ge(s["dve_lt"], 2 * i + 1)
                pe_x0t(eng, i + 1, 1)
            if head:
                pe_o(eng, i, 3)
            if tail:
                e1 = pe_expert(eng, p, 1)
                pe_out(eng, p, 1, 0, e1)
            if head:
                pe_lt(eng, i, 1, nxt)
            if tail:
                pe_out(eng, p, 1, 1, e1)
            if nxt:
                pe_low(eng, i + 1)
            if head:
                pe_up(eng, i, 1)

        def pe_prologue(eng):
            eng.wait_ge(s["ids_in"], 48)
            eng.wait_ge(s["ident_ok"], 2)
            eng.wait_ge(s["ewi_in"], 32)
            for k in range(DT):
                m = eng.transpose(mbank[0][:, k * P:(k + 1) * P], ewia_raw[:, k * P:(k + 1) * P], ident[:])
            m.then_inc(s["pe_eia"], 1)
            eng.wait_ge(s["ewib_ok"], 1)
            for t in range(FT):
                m = eng.transpose(mbank[1 + t // 4][:, (t % 4) * P:(t % 4 + 1) * P],
                                  ewib_s[:, t], ident[:])
                if t % 4 == 3:
                    m.then_inc(s["pe_eib"], 1)
            eng.wait_ge(s["cia_in"], 32)
            for t in range(FT):
                m = eng.transpose(obank[t // 4][0:R, (t % 4) * P:(t % 4 + 1) * P],
                                  cib_raw[:, t * R:(t + 1) * R], ident[:])
            m.then_inc(s["pe_cib"], 1)
            eng.wait_ge(s["x0_in"], 16)
            pe_x0t(eng, 0, 0)
            pe_x0t(eng, 0, 1)
            eng.wait_ge(s["wi_in"], 16)
            eng.wait_ge(s["act_cib"], 1)
            for n, bank in enumerate(WI_BANKS):
                k, a = divmod(n, 2)
                if n == 1:
                    eng.wait_ge(s["dve_eia"], DT)
                if n == 2:
                    eng.wait_ge(s["dve_eib"], 2)
                eng.matmul(bank[:, :], cia_raw[:, k * P:(k + 1) * P], cibT[:, a * 512:(a + 1) * 512],
                           start=True, stop=False, skip_group_check=True)
                for t in range(4):
                    m = eng.matmul(bank[:, t * P:(t + 1) * P], wi_raw[:, 4 * a + t, k * P:(k + 1) * P],
                                   ident[:], start=False, stop=True, skip_group_check=True)
                m.then_inc(s["pe_wi"], 1)
            eng.wait_ge(s["coa_in"], 32)
            for t in range(DT):
                m = eng.transpose(obank[0][0:R, t * P:(t + 1) * P], cob_raw[:, t * R:(t + 1) * R], ident[:])
            m.then_inc(s["pe_cob"], 1)
            eng.wait_ge(s["ewo_in"], 32)
            eng.wait_ge(s["ewob_ok"], 1)
            for t in range(DT):
                m = eng.transpose(obank[1][:, t * P:(t + 1) * P], ewob_s[:, t], ident[:])
            m.then_inc(s["pe_eob"], 1)
            for a, bank in enumerate(EOA_BANKS):
                eng.wait_ge(s["dve_wi"], 1 + a)
                for t in range(4):
                    f = 4 * a + t
                    m = eng.transpose(bank[:, t * P:(t + 1) * P], ewoa_raw[:, f * P:(f + 1) * P], ident[:])
                m.then_inc(s["pe_eoa"], 1)
            eng.wait_ge(s["wo_in"], 16)
            eng.wait_ge(s["act_cob"], 1)
            eng.wait_ge(s["dve_eob"], 1)
            for f in range(FT):
                if f >= 2:
                    eng.wait_ge(s["dve_wo"], f - 1)
                o = obank[f % 2]
                eng.matmul(o[:, 0:D], coa_raw[:, f * P:(f + 1) * P], cobT[:], start=True, stop=False,
                           skip_group_check=True)
                for t in range(DT):
                    m = eng.matmul(o[:, t * P:(t + 1) * P], wo_raw[:, t, f * P:(f + 1) * P], ident[:],
                                   start=False, stop=True, skip_group_check=True)
                m.then_inc(s["pe_wo"], 1)
            pe_low(eng, 0)

        def act_x0t(eng, i, j):
            eng.wait_ge(s["pe_x0t"], 2 * i + j + 1)
            nc.scalar.copy(x0T_h[:, :, j * S:(j + 1) * S],
                           hbank[1 - j][:, :].rearrange("p (k n) -> p k n", k=DT)).then_inc(s["act_x0t"], 1)

        def act_body(eng, i, head, tail, nxt):
            p = i - 1
            copy = nc.scalar.copy

            def a_h(f):
                eng.wait_ge(s["pe_h"], FT * i + f + 1)
                nc.scalar.activation(hT_h[:, f], H_BANKS[f % 4][:, :], ACT.Relu).then_inc(s["act_h"], 1)

            def a_lt(j):
                eng.wait_ge(s["pe_lt"], 2 * i + j + 1)
                copy(lowT[:, j * ST:(j + 1) * ST],
                     hbank[0][0:4 * R, 0:S].rearrange("p (t n) -> p t n", t=ST)).then_inc(s["act_lt"], 1)

            def a_x1t(j):
                eng.wait_ge(s["pe_x1t"], 2 * p + j + 1)
                copy(x1T_h[:, :, j * S:(j + 1) * S],
                     mbank[j][:, :].rearrange("p (k n) -> p k n", k=DT)).then_inc(s["act_x1t"], 1)

            def a_exp(j):
                eng.wait_ge(s["dve_arg"], 4 * p + 2 * j + 2)
                nc.scalar.activation(terms[:, j], terms[:, j], ACT.Exp, scale=-1.0).then_inc(s["act_exp"], 1)
                eng.wait_ge(s["act_exp"], 2 * p + j + 1)
                copy(p_h[:, j], terms[:, j]).then_inc(s["act_ph"], 1)

            def a_x2h(j):
                eng.wait_ge(s["dve_x2"], 4 * p + 2 * j + 2)
                copy(x2_h[:, j], x2[:, j]).then_inc(s["act_x2h"], 1)

            def a_ut(j):
                eng.wait_ge(s["pe_ut"], 2 * p + j + 1)
                copy(x1T_h[:, :, j * S:(j + 1) * S],
                     mbank[UT_BANK[j]][:, :].rearrange("p (k n) -> p k n", k=DT)).then_inc(s["act_ut"], 1)

            def a_w2(e):
                eng.wait_ge(s["pe_w2"], e + 1)
                copy(w2T_h[:, e], mbank[e % 3][:, :].rearrange("p (k n) -> p k n", k=DT)
                     ).then_inc(s["act_w2"], 1)

            if head and not tail:
                for f in range(FT):
                    a_h(f)
                    a_w2(f)
                head_tiles = ()
            else:
                head_tiles = range(FT) if head else ()
            if tail:
                a_x1t(0)
            if 0 in head_tiles:
                a_h(0)
            if tail:
                a_x1t(1)
            if 1 in head_tiles:
                a_h(1)
            if tail:
                eng.wait_ge(s["pe_tt"], 2 * p + 1)
                copy(tT_h[:, 0], mbank[2][:, :].rearrange("p (k n) -> p k n", k=ST)).then_inc(s["act_tt"], 1)
                eng.wait_ge(s["pe_a"], p + 1)
                nc.scalar.activation(th[:], mbank[0][:, :], ACT.Tanh, bias=b1_c[:]).then_inc(s["act_tanh"], 1)
                eng.wait_ge(s["act_tanh"], p + 1)
                copy(tstk[:], th[:]).then_inc(s["act_th"], 1)
            if 2 in head_tiles:
                a_h(2)
            if tail:
                eng.wait_ge(s["pe_tt"], 2 * p + 2)
                copy(tT_h[:, 1], mbank[1][:, :].rearrange("p (k n) -> p k n", k=ST)).then_inc(s["act_tt"], 1)
                copy(x1_h[:, 0, :, 0:D], x1[:, 0]).then_inc(s["act_x1h"], 1)
            if 3 in head_tiles:
                a_h(3)
            if tail:
                eng.wait_ge(s["pe_sr"], p + 1)
                copy(th[:], mbank[2][:, :]).then_inc(s["act_srow"], 1)
                copy(x1_h[:, 1, :, 0:D], x1[:, 1]).then_inc(s["act_x1h"], 1)
            if 4 in head_tiles:
                a_h(4)
                a_h(5)
                a_h(6)
            if tail:
                a_exp(0)
            if 7 in head_tiles:
                a_h(7)
            if tail:
                a_exp(1)
                a_x2h(0)
                a_x2h(1)
                a_ut(0)
            if head:
                a_lt(0)
            if tail:
                a_ut(1)
            if nxt:
                act_x0t(eng, i + 1, 0)
                act_x0t(eng, i + 1, 1)
            if head:
                a_lt(1)
            if nxt:
                eng.wait_ge(s["pe_low"], i + 2)
                copy(low[:], hbank[1][:, :]).then_inc(s["act_low"], 1)

        def act_prologue(eng):
            copy, mul = nc.scalar.copy, nc.scalar.mul
            eng.wait_ge(s["pe_eia"], 1)
            for k in range(DT):
                src = mbank[0][:, k * P:(k + 1) * P].rearrange("p (e o r) -> p e o r", e=E, o=1)
                for c in (0, 4 * R):
                    m = copy(eia_st[:, :, k, c:c + 2 * R].rearrange("p e (g r) -> p e g r", g=2),
                             src.to_broadcast([P, E, 2, R]))
                m.then_inc(s["act_eia"], 1)
            for a in range(2):
                eng.wait_ge(s["pe_eib"], 1 + a)
                dst = eib_st[:, 0].rearrange("p (n t) -> p t n", t=FT)
                mul(dst[:, 4 * a:4 * a + 4], mbank[1 + a][:, :].rearrange("p (t n) -> p t n", t=4),
                    ALPHA).then_inc(s["act_eib"], 1)
            eng.wait_ge(s["pe_cib"], 1)
            dst = cibT[:].rearrange("r (n t) -> r t n", t=FT)
            for a in range(2):
                m = mul(dst[:, 4 * a:4 * a + 4], obank[a][0:R, :].rearrange("r (t n) -> r t n", t=4), ALPHA)
            m.then_inc(s["act_cib"], 1)
            act_x0t(eng, 0, 0)
            act_x0t(eng, 0, 1)
            for n, bank in enumerate(WI_BANKS):
                k, a = divmod(n, 2)
                eng.wait_ge(s["pe_wi"], 1 + n)
                copy(wiT_h[:, k, a * 512:(a + 1) * 512], bank[:, :]).then_inc(s["act_wi"], 1)
            eng.wait_ge(s["pe_cob"], 1)
            mul(cobT[:].rearrange("r (n t) -> r t n", t=DT),
                obank[0][0:R, 0:D].rearrange("r (t n) -> r t n", t=DT), ALPHA).then_inc(s["act_cob"], 1)
            eng.wait_ge(s["pe_eob"], 1)
            mul(eob_st[:, 0].rearrange("p (n t) -> p t n", t=DT),
                obank[1][:, 0:D].rearrange("p (t n) -> p t n", t=DT), ALPHA).then_inc(s["act_eob"], 1)
            for a, bank in enumerate(EOA_BANKS):
                eng.wait_ge(s["pe_eoa"], 1 + a)
                copy(ewoT_h[:, 4 * a:4 * a + 4], bank[:, :].rearrange("p (t n) -> p t n", t=4)
                     ).then_inc(s["act_eoa"], 1)
            for f in range(FT):
                eng.wait_ge(s["pe_wo"], 1 + f)
                copy(woT_h[:, f, R:R + D], obank[f % 2][:, 0:D]).then_inc(s["act_wo"], 1)
            eng.wait_ge(s["pe_low"], 1)
            copy(low[:], hbank[1][:, :]).then_inc(s["act_low"], 1)
            eng.wait_ge(s["small_in"], 80)

        def minus(dst, src, hi):
            return nc.vector.tensor_tensor(dst, src, hi.bitcast(F32), ALU.subtract)

        def lo_T(lo, hi, bank, j):
            c = slice(j * S, (j + 1) * S)
            return minus(lo[:, :, c], bank[:, :].rearrange("p (k n) -> p k n", k=DT), hi[:, :, c])

        def dve_x0t(eng, i, j):
            eng.wait_ge(s["act_x0t"], 2 * i + j + 1)
            lo_T(x0T_l, x0T_h, hbank[1 - j], j).then_inc(s["dve_x0t"], 1)

        def dve_body(eng, i, head, tail, nxt):
            p = i - 1

            def d_h(f):
                eng.wait_ge(s["act_h"], FT * i + f + 1)
                nc.vector.scalar_tensor_tensor(
                    out=hT_l[:, f], in0=H_BANKS[f % 4][:, :], scalar=0.0, in1=hT_h[:, f].bitcast(F32),
                    op0=ALU.max, op1=ALU.subtract).then_inc(s["dve_h"], 1)

            def d_x1t(j):
                eng.wait_ge(s["act_x1t"], 2 * p + j + 1)
                lo_T(x1T_l, x1T_h, mbank[j], j).then_inc(s["dve_x1t"], 1)

            def d_tt(j):
                eng.wait_ge(s["act_tt"], 2 * p + j + 1)
                minus(tT_l[:, j], mbank[2 - j][:, :].rearrange("p (k n) -> p k n", k=ST),
                      tT_h[:, j]).then_inc(s["dve_tt"], 1)

            def d_lowrep(n):
                j = n // ST
                eng.wait_ge(s["pe_o"], 4 * i + n + 1)
                src = obank[O_OF[n]][:, O_LOW[j]:O_LOW[j] + R].rearrange("p (o r) -> p o r", o=1)
                nc.vector.tensor_copy(low_o[:, n], src.to_broadcast([P, G, R])).then_inc(s["dve_lowrep"], 1)

            def d_lt(j):
                eng.wait_ge(s["act_lt"], 2 * i + j + 1)
                q = slice(2 * R, 4 * R)
                minus(lowT[q, j * ST:(j + 1) * ST], hbank[0][q, 0:S].rearrange("p (t n) -> p t n", t=ST),
                      lowT[q, j * ST:(j + 1) * ST]).then_inc(s["dve_lt"], 1)

            def d_x1(n):
                j, t = divmod(n, ST)
                eng.wait_ge(s["pe_up"], 4 * i + n + 1)
                if t == 0:
                    eng.wait_ge(s[f"xres_in{j}"], 16 * (i + 1))
                nc.vector.tensor_tensor(x1[:, j, t], obank[O_OF[n]][:, O_W[j]:O_W[j] + D], x1[:, j, t],
                                        ALU.add).then_inc(s["dve_x1"], 1)

            def d_pre(j):
                if j == 0:
                    eng.wait_ge(s["act_srow"], p + 1)
                else:
                    eng.wait_ge(s["dve_max"], 6 * p + 3)
                row = th[:, j * S:(j + 1) * S]
                nc.vector.tensor_tensor_scan(pre_max[:, S + 1:], row, row, -BIG, ALU.max,
                                             ALU.max).then_inc(s["dve_max"], 1)

            def d_suf(j):
                row = th[:, (j + 1) * S - 1:j * S - 1:-1] if j else th[:, S - 1::-1]
                nc.vector.tensor_tensor_scan(suf_max[:, S - 1::-1], row, row, -BIG, ALU.max,
                                             ALU.max).then_inc(s["dve_max"], 1)

            def d_score_cols(j):
                for l in range(ST):
                    n = ST * j + l
                    nc.vector.tensor_tensor_reduce(
                        out=terms[:, j, l, 0:P], in0=th[:, n * P:(n + 1) * P], in1=ident[:], scale=1.0,
                        scalar=0.0, op0=ALU.mult, op1=ALU.add, accum_out=s_col[:, n:n + 1]
                    ).then_inc(s["dve_sc"], 1)

            def d_kind(j):
                kind = eng.value_load(ids[0:1, 1, bass.ds(2 * p + j, 1)], min_val=0, max_val=2)
                a = eng.value_load(pre_at[0:1, bass.ds(kind, 1)], min_val=0, max_val=S + 1)
                b = eng.value_load(suf_at[0:1, bass.ds(kind, 1)], min_val=0, max_val=S + 1)
                return kind, a, b

            def d_arg(j, at):
                kind, a, b = at
                eng.wait_ge(s["dve_max"], 6 * p + 3 * j + 2)
                if j:
                    eng.wait_ge(s["dve_arg"], 4 * p + 2)
                nc.vector.tensor_tensor(mrow[:], pre_max[:, bass.ds(a, S)], suf_max[:, bass.ds(b, S)],
                                        ALU.max).then_inc(s["dve_max"], 1)
                eng.wait_ge(s["dve_sc"], 4 * p + 2 * j + 2)
                eng.wait_ge(s["dve_max"], 6 * p + 3 * j + 3)
                for l in range(ST):
                    mask = mask_big[:, bass.ds(kind, 1), l].rearrange("p o n -> p (o n)")
                    nc.vector.scalar_tensor_tensor(
                        out=terms[:, j, l], in0=mrow[:], scalar=s_col[:, ST * j + l:ST * j + l + 1], in1=mask,
                        op0=ALU.subtract, op1=ALU.max).then_inc(s["dve_arg"], 1)

            def d_x2(j, at):
                kind = at[0]
                tiles = [(t, ST * j + t, mbank[POOL_BANK[ST * j + t]]) for t in range(ST)]
                for t, n, bank in tiles:
                    eng.wait_ge(s["pe_pool"], 4 * p + n + 1)
                    nc.vector.tensor_tensor(zc[:, n:n + 1], bank[:, D:D + 1], cnt[:, bass.ds(kind, 1), t],
                                            ALU.mult).then_inc(s["dve_z"], 1)
                c = slice(ST * j, ST * (j + 1))
                eng.wait_ge(s["dve_z"], 6 * p + 3 * j + 2)
                nc.vector.reciprocal(rz[:, c], zc[:, c]).then_inc(s["dve_z"], 1)
                if j == 0:
                    eng.wait_ge(s["out_free"], 32 * p + 32)
                eng.wait_ge(s["dve_z"], 6 * p + 3 * j + 3)
                for t, n, bank in tiles:
                    nc.vector.scalar_tensor_tensor(
                        out=x2[:, j, t], in0=bank[:, 0:D], scalar=rz[:, n:n + 1], in1=x1[:, j, t],
                        op0=ALU.mult, op1=ALU.add).then_inc(s["dve_x2"], 1)

            def d_rowsum(j):
                eng.wait_ge(s["pool_ti"], 4 * p + 2 * j + 2)
                nc.vector.tensor_reduce(rowsum[:, ST * j:ST * (j + 1)], t_raw[:, j], AX.X, ALU.add
                                        ).then_inc(s["dve_rs"], 1)

            def d_ut(j):
                eng.wait_ge(s["act_ut"], 2 * p + j + 1)
                lo_T(x1T_l, x1T_h, mbank[UT_BANK[j]], j).then_inc(s["dve_ut"], 1)

            def d_out(j):
                eng.wait_ge(s["pe_out"], 4 * p + 2 * j + 2)
                if j == 0:
                    eng.wait_ge(s["bias_in"], 32 * (p + 1))
                    eng.wait_ge(s["dve_rs"], 2 * p + 2)
                    eng.wait_ge(s["pool_x2l"], 2 * p + 2)
                for t in range(ST):
                    m = nc.vector.scalar_tensor_tensor(
                        out=x2[:, j, t], in0=bias_t[:, j], scalar=rowsum[:, ST * j + t:ST * j + t + 1],
                        in1=mbank[1 + j][:, t * D:(t + 1) * D], op0=ALU.mult, op1=ALU.add)
                m.then_inc(s["dve_out"], 1)

            def d_w2(e):
                eng.wait_ge(s["act_w2"], e + 1)
                minus(w2T_l[:, e], mbank[e % 3][:, :].rearrange("p (k n) -> p k n", k=DT),
                      w2T_h[:, e]).then_inc(s["dve_w2"], 1)

            if head and not tail:
                for f in range(FT):
                    d_h(f)
                    d_w2(f)
                head_tiles = ()
            else:
                head_tiles = range(FT) if head else ()
            if tail:
                d_x1t(0)
            if 0 in head_tiles:
                d_h(0)
            if tail:
                d_x1t(1)
            if 1 in head_tiles:
                d_h(1)
            if tail:
                d_tt(0)
                at0 = d_kind(0)
                eng.wait_ge(s["act_th"], p + 1)
                q = slice(A, P)
                minus(tstk[q], th[q], tstk[q]).then_inc(s["dve_tstk"], 1)
            if 2 in head_tiles:
                d_h(2)
            if tail:
                d_tt(1)
                at1 = d_kind(1)
            if 3 in head_tiles:
                d_h(3)
            if tail:
                d_pre(0)
                d_suf(0)
            if 4 in head_tiles:
                d_h(4)
            if tail:
                d_score_cols(0)
                d_arg(0, at0)
            if 5 in head_tiles:
                d_h(5)
            if tail:
                d_pre(1)
                d_suf(1)
            if 6 in head_tiles:
                d_h(6)
            if tail:
                d_score_cols(1)
            if 7 in head_tiles:
                d_h(7)
            if tail:
                d_arg(1, at1)
            if head:
                d_lowrep(0)
            if tail:
                d_rowsum(0)
                d_rowsum(1)
                d_x2(0, at0)
            if head:
                d_lowrep(1)
            if tail:
                d_x2(1, at1)
                d_ut(0)
            if head:
                d_lt(0)
                d_lowrep(2)
                d_x1(0)
                d_x1(1)
            if tail:
                d_ut(1)
                d_out(0)
            if nxt:
                dve_x0t(eng, i + 1, 0)
                dve_x0t(eng, i + 1, 1)
            if head:
                d_lowrep(3)
                d_lt(1)
                d_x1(2)
                d_x1(3)
            if nxt:
                dve_low(eng, i + 1)
            if tail:
                d_out(1)

        def dve_low(eng, i):
            eng.wait_ge(s["act_low"], i + 1)
            q = slice(4 * R, P)
            minus(low[q], hbank[1][q, :], low[q]).then_inc(s["dve_low"], 1)

        def dve_prologue(eng):
            eng.wait_ge(s["ids_in"], 48)
            eng.wait_ge(s["ewi_in"], 32)
            nc.vector.tensor_copy(ewib_s[:].rearrange("p t (e r) -> p t e r", r=R),
                                  ewib_raw[:].rearrange("p e (t r) -> p t e r", r=R)).then_inc(s["ewib_ok"], 1)
            for k in range(DT):
                eng.wait_ge(s["act_eia"], DT)
                src = mbank[0][:, k * P:(k + 1) * P].rearrange("p (e o r) -> p e o r", e=E, o=1)
                for c in (0, 4 * R):
                    hi, lo = (eia_st[:, :, k, c + n * 2 * R:c + (n + 1) * 2 * R].rearrange(
                        "p e (g r) -> p e g r", g=2) for n in range(2))
                    m = minus(lo, src.to_broadcast([P, E, 2, R]), hi)
                m.then_inc(s["dve_eia"], 1)
            for a in range(2):
                eng.wait_ge(s["act_eib"], 1 + a)
                hi = eib_st[:, 0].rearrange("p (n t) -> p t n", t=FT)[:, 4 * a:4 * a + 4]
                lo = eib_st[:, 1].rearrange("p (n t) -> p t n", t=FT)[:, 4 * a:4 * a + 4]
                nc.vector.scalar_tensor_tensor(
                    out=lo, in0=mbank[1 + a][:, :].rearrange("p (t n) -> p t n", t=4), scalar=ALPHA,
                    in1=hi.bitcast(F32), op0=ALU.mult, op1=ALU.subtract).then_inc(s["dve_eib"], 1)
            dve_x0t(eng, 0, 0)
            dve_x0t(eng, 0, 1)
            for n, bank in enumerate(WI_BANKS):
                k, a = divmod(n, 2)
                eng.wait_ge(s["act_wi"], 1 + n)
                c = slice(a * 512, (a + 1) * 512)
                minus(wiT_l[:, k, c], bank[:, :], wiT_h[:, k, c]).then_inc(s["dve_wi"], 1)
            eng.wait_ge(s["ewo_in"], 32)
            nc.vector.tensor_copy(ewob_s[:].rearrange("p t (e r) -> p t e r", r=R),
                                  ewob_raw[:].rearrange("p e (t r) -> p t e r", r=R)).then_inc(s["ewob_ok"], 1)
            eng.wait_ge(s["act_eob"], 1)
            hi, lo = (eob_st[:, n].rearrange("p (n t) -> p t n", t=DT) for n in range(2))
            nc.vector.scalar_tensor_tensor(
                out=lo, in0=obank[1][:, 0:D].rearrange("p (t n) -> p t n", t=DT), scalar=ALPHA,
                in1=hi.bitcast(F32), op0=ALU.mult, op1=ALU.subtract).then_inc(s["dve_eob"], 1)
            for a, bank in enumerate(EOA_BANKS):
                eng.wait_ge(s["act_eoa"], 1 + a)
                minus(ewoT_l[:, 4 * a:4 * a + 4], bank[:, :].rearrange("p (t n) -> p t n", t=4),
                      ewoT_h[:, 4 * a:4 * a + 4]).then_inc(s["dve_eoa"], 1)
            for f in range(FT):
                eng.wait_ge(s["act_wo"], 1 + f)
                minus(woT_l[:, f, R:R + D], obank[f % 2][:, 0:D], woT_h[:, f, R:R + D]).then_inc(s["dve_wo"], 1)
            dve_low(eng, 0)
            eng.wait_ge(s["small_in"], 80)
            w1 = w1_raw[:].rearrange("p k (o a) -> p k o a", o=1).to_broadcast([P, DT, 2, A])
            w1h, w1l = (t[:].rearrange("p k (o a) -> p k o a", o=2) for t in (w1_h, w1_l))
            nc.vector.tensor_copy(w1h, w1).then_inc(s["small_ok"], 1)
            nc.vector.tensor_copy(v_h[:], v_c[:].to_broadcast([P, P])).then_inc(s["small_ok"], 1)
            eng.wait_ge(s["small_ok"], 2)
            minus(w1l, w1, w1h).then_inc(s["small_ok"], 1)
            minus(v_l[:], v_c[:].to_broadcast([P, P]), v_h[:]).then_inc(s["small_ok"], 1)
            eng.wait_ge(s["masks_ok"], 3)
            eng.wait_ge(s["cnt_ok"], 3)
            nc.vector.tensor_copy(cnt[:], cnt_i[:]).then_inc(s["cnt_ok"], 1)
            eng.wait_ge(s["cnt_ok"], 4)
            eng.sem_inc(s["dve_out"], 1)

        def minus_pool(dst, src, hi):
            return nc.gpsimd.tensor_tensor(dst, src, hi.bitcast(F32), ALU.subtract)

        def pool_prologue(eng):
            eng.memset(ident[:], 0.0).then_inc(s["ident_ok"], 1)
            eng.wait_ge(s["ident_ok"], 1)
            eng.affine_select(out=ident[:], in_=ident[:], compare_op=ALU.not_equal, fill=1.0, base=0,
                              pattern=[[-1, P]], channel_multiplier=1).then_inc(s["ident_ok"], 1)
            for k, (a, b) in enumerate(((S + 1, S + 1), (0, 0), (S, 1))):
                eng.memset(pre_at[0:1, k:k + 1], a)
                eng.memset(suf_at[0:1, k:k + 1], b)
            eng.memset(pre_max[:, 0:S + 1], -BIG)
            eng.memset(suf_max[:, S:], -BIG)
            eng.memset(mask_big[:], 0.0).then_inc(s["masks_ok"], 1)
            eng.iota(cnt_i[:, 0], pattern=[[P, ST]], base=1, channel_multiplier=1).then_inc(s["cnt_ok"], 1)
            eng.iota(cnt_i[:, 1], pattern=[[-P, ST]], base=S, channel_multiplier=-1).then_inc(s["cnt_ok"], 1)
            eng.iota(cnt_i[:, 2], pattern=[[0, ST]], base=S - 1, channel_multiplier=0).then_inc(s["cnt_ok"], 1)
            eng.wait_ge(s["masks_ok"], 1)
            for k, (sign, op) in enumerate(((1, ALU.is_ge), (-1, ALU.is_ge), (1, ALU.not_equal))):
                m = eng.affine_select(out=mask_big[:, k], in_=mask_big[:, k], compare_op=op, fill=BIG, base=0,
                                      pattern=[[-sign * P, ST], [sign, S]], channel_multiplier=-sign)
            m.then_inc(s["masks_ok"], 2)
            eng.wait_ge(s["ids_in"], 48)
            eng.wait_ge(s["w2_in"], 16)
            for t in range(DT):
                d = w2_raw[:, :, t, t * P:(t + 1) * P]
                nc.gpsimd.tensor_tensor(d, d, ident[:].rearrange("p (o n) -> p o n", o=1).to_broadcast([P, E, P]),
                                        ALU.add).then_inc(s["w2_ok"], 1)

        def pool_body(eng, i, head, tail, nxt):
            p = i - 1
            if head and not tail:
                eng.wait_ge(s["dve_eoa"], 2)
            if tail:
                eng.wait_ge(s["t_in"], 32 * (p + 1))
                for j in range(2):
                    for t in range(ST):
                        d = t_raw[:, j, t, t * P:(t + 1) * P]
                        nc.gpsimd.tensor_tensor(d, d, ident[:], ALU.add).then_inc(s["pool_ti"], 1)
                eng.wait_ge(s["dve_x1"], 4 * p + 4)
                for j in range(2):
                    eng.wait_ge(s["act_x1h"], 2 * p + j + 1)
                    minus_pool(x1_l[:, j, :, 0:D], x1[:, j], x1_h[:, j, :, 0:D]).then_inc(s["pool_x1l"], 1)
            if head:
                for j in range(2):
                    e = eng.value_load(ids[0:1, 0, bass.ds(2 * i + j, 1)], min_val=0, max_val=E - 1)
                    if j == 0 and tail:
                        eng.wait_ge(s["pe_o"], 4 * i)
                    c = slice(j * (R + D), j * (R + D) + R)
                    for src, dst in ((ewoT_h, woT_h), (ewoT_l, woT_l)):
                        nc.gpsimd.tensor_copy(dst[:, :, c], src[:, :, bass.ds(e * R, R)].bitcast(F32)
                                              ).then_inc(s["pool_eoa"], 1)
            if head and not tail:
                eng.wait_ge(s["pe_w2"], E)
                eng.memset(x1_h[:, :, :, D:].bitcast(F32), 1.0).then_inc(s["ones_ok"], 1)
                eng.memset(x1_l[:, :, :, D:].bitcast(F32), 0.0).then_inc(s["ones_ok"], 1)
            if tail:
                for j in range(2):
                    eng.wait_ge(s["act_ph"], 2 * p + j + 1)
                    minus_pool(p_l[:, j], terms[:, j], p_h[:, j]).then_inc(s["pool_pl"], 1)
                for j in range(2):
                    eng.wait_ge(s["act_x2h"], 2 * p + j + 1)
                    minus_pool(x2_l[:, j], x2[:, j], x2_h[:, j]).then_inc(s["pool_x2l"], 1)

        def run(eng, prologue, body):
            prologue(eng)
            body(eng, 0, True, False, True)
            with eng.Fori(1, PAIRS - 1) as i:
                body(eng, i, True, True, True)
            body(eng, PAIRS - 1, True, True, False)
            body(eng, PAIRS, False, True, False)

        block = ctx.enter_context(nc.Block())

        @block.sync
        def _(eng):
            run(eng, sp_prologue, sp_body)
            eng.wait_ge(s["out_free"], 32 * PAIRS + 32)

        @block.tensor
        def _(eng):
            run(eng, pe_prologue, pe_body)

        @block.scalar
        def _(eng):
            run(eng, act_prologue, act_body)

        @block.vector
        def _(eng):
            run(eng, dve_prologue, dve_body)

        @block.gpsimd
        def _(eng):
            run(eng, pool_prologue, pool_body)


_INS = ['x', 'itok_B_0_7', 'itok_B_0_2', 'itok_B_1_98', 'L0_cond_wi', 'L0_cond_wo', 'L0_cond_common_wi_a',
        'L0_cond_common_wi_b', 'L0_cond_common_wo_a', 'L0_cond_common_wo_b', 'L0_cond_experts_wi_a',
        'L0_cond_experts_wi_b', 'L0_cond_experts_wo_a', 'L0_cond_experts_wo_b', 'L1_cond_W1', 'L1_cond_b1',
        'L1_cond_v', 'L2_cond_weight', 'L2_cond_bias', 'L3_cond_T']


def kernel(**inputs):
    import numpy as _np
    import concourse.bacc as _bacc
    from concourse import mybir as _mybir
    from concourse.bass_utils import run_bass_kernel_spmd as _run

    nc = _bacc.Bacc("TRN2", target_bir_lowering=False, num_devices=1)
    arrays, args = {}, []
    for name in _INS:
        a = _np.ascontiguousarray(inputs[name])
        arrays[f"in_{name}_dram"] = a
        args.append(nc.dram_tensor(f"in_{name}_dram", a.shape, _mybir.dt.from_np(a.dtype), kind="ExternalInput").ap())
    shape = arrays["in_x_dram"].shape
    args.append(nc.dram_tensor("out_0_dram", shape, _mybir.dt.from_np(_np.dtype("float32")), kind="ExternalOutput").ap())
    build(nc, *args)
    r = _run(nc, [arrays], core_ids=[0])
    return r.results[0]["out_0_dram"]
```

```python
from contextlib import ExitStack

import concourse.bass as bass
from concourse import mybir

F32 = mybir.dt.float32
F32R = mybir.dt.float32r
BF16 = mybir.dt.bfloat16
I32 = mybir.dt.int32
ALU = mybir.AluOpType
AX = mybir.AxisListType
ACT = mybir.ActivationFunctionType

P = 128
BIG = 1.0e30
ALPHA = 2.0


class Places:

    def __init__(self, xT, x1, x2, x1t, tt, parts, a, sr, pool, ut, out):
        self.xT, self.x1, self.x2 = xT, x1, x2
        self.x1t, self.tt, self.parts, self.a, self.sr = x1t, tt, parts, a, sr
        self.pool, self.ut, self.out = pool, ut, out


class Steps:
    pass


def build(nc, x, expert_id, mask_id, step_id, wi, wo, cwi_a, cwi_b, cwo_a, cwo_b,
          ewi_a, ewi_b, ewo_a, ewo_b, W1, b1, v, W2, bias2, T, out):
    B, S, D = x.shape
    F = wi.shape[0]
    E, R, _ = ewi_a.shape
    A = W1.shape[1]
    ST, DT, FT = S // P, D // P, F // P
    PAIRS = B // 2
    N2 = 2 * S
    G = P // R
    assert (ST, DT, 2 * A, E * R, G) == (2, 2, P, P, 8)

    with ExitStack() as ctx:
        def sb(name, shape, dt=F32):
            return ctx.enter_context(nc.sbuf_tensor(name, shape, dt))

        def sem(name):
            return ctx.enter_context(nc.semaphore(name))

        ids = sb("ids", [1, 3, B], I32)
        ident = sb("ident", [P, P])
        wiT_h = sb("wiT_h", [P, DT, F], F32R)
        wiT_l = sb("wiT_l", [P, DT, F], F32R)
        woT_h = sb("woT_h", [P, FT, R + D + R], F32R)
        woT_l = sb("woT_l", [P, FT, R + D + R], F32R)
        ewoT_h = sb("ewoT_h", [P, FT, E * R], F32R)
        ewoT_l = sb("ewoT_l", [P, FT, E * R], F32R)
        w1_h = sb("w1_h", [P, DT, P], F32R)
        w1_l = sb("w1_l", [P, DT, P], F32R)
        v_h = sb("v_h", [P, P], F32R)
        v_l = sb("v_l", [P, P], F32R)
        b1_c = sb("b1_c", [P, 1])
        v_c = sb("v_c", [P, 1])
        mask_big = sb("mask_big", [P, 3, ST, S], BF16)
        cnt = sb("cnt", [P, 3, ST])
        cnt_i = sb("cnt_i", [P, 3, ST], I32)
        pre_at = sb("pre_at", [1, 3], I32)
        suf_at = sb("suf_at", [1, 3], I32)
        pre_max = sb("pre_max", [P, S + 1 + S])
        suf_max = sb("suf_max", [P, S + S + 1])

        raw = ExitStack()

        def rb(name, shape, dt=F32):
            return raw.enter_context(nc.sbuf_tensor(name, shape, dt))

        wi_raw = rb("wi_raw", [P, FT, D])
        cia_raw = rb("cia_raw", [P, D])
        cia_st = rb("cia_st", [P, D], F32R)
        cib_raw = rb("cib_raw", [P, FT * R])
        cib_s = rb("cib_s", [P, FT, G * R])
        cibT = rb("cibT", [P, F], F32R)
        ewia_raw = rb("ewia_raw", [P, D])
        ewib_raw = rb("ewib_raw", [P, E, FT * R])
        ewib_s = rb("ewib_s", [P, FT, E * R])
        coa_st = rb("coa_st", [P, F], F32R)
        raw.close()
        w2T_h = sb("w2T_h", [P, E, DT, D], F32R)
        w2T_l = sb("w2T_l", [P, E, DT, D], F32R)

        w2_raw = rb("w2_raw", [P, E, DT, D])
        wo_raw = rb("wo_raw", [P, DT, F])
        coa_raw = rb("coa_raw", [P, F])
        cob_raw = rb("cob_raw", [P, DT * R])
        cob_s = rb("cob_s", [P, DT, G * R])
        cobT = rb("cobT", [P, D], F32R)
        ewoa_raw = rb("ewoa_raw", [P, F])
        ewob_raw = rb("ewob_raw", [P, E, DT * R])
        ewob_s = rb("ewob_s", [P, DT, E * R])
        w1_raw = rb("w1_raw", [P, DT, A])
        eob_st = rb("eob_st", [P, 2, D], F32R)
        eia_st = rb("eia_st", [P, E, DT, P], F32R)
        eib_st = rb("eib_st", [P, 2, F], F32R)
        raw.close()

        x1T_h = sb("x1T_h", [P, DT, N2], F32R)
        x1T_l = sb("x1T_l", [P, DT, N2], F32R)
        th = sb("th", [P, N2])
        tstk = sb("tstk", [P, N2], F32R)
        terms = sb("terms", [P, 2, ST, S])
        p_h = sb("p_h", [P, 2, ST, S], F32R)
        p_l = sb("p_l", [P, 2, ST, S], F32R)
        x1_h = sb("x1_h", [P, 2, ST, D + 2], F32R)
        x1_l = sb("x1_l", [P, 2, ST, D + 2], F32R)
        x2 = sb("x2", [P, 2, ST, D])
        t_raw = sb("t_raw", [P, 2, ST, S])
        tT_h = sb("tT_h", [P, 2, ST, S], F32R)
        tT_l = sb("tT_l", [P, 2, ST, S], F32R)
        hT_h = sb("hT_h", [P, FT, N2], F32R)
        hT_l = sb("hT_l", [P, FT, N2], F32R)
        x2_h, x2_l = p_h, p_l
        x0 = sb("x0", [P, 2, ST, D])
        x0T_h = sb("x0T_h", [P, DT, N2], F32R)
        x0T_l = sb("x0T_l", [P, DT, N2], F32R)
        eia = sb("eia", [P, 2, DT, P], F32R)
        eib = sb("eib", [P, 2, F], F32R)
        low = sb("low", [P, N2], F32R)
        eob = sb("eob", [4 * R, 2, D], F32R)
        low_o = sb("low_o", [P, 2 * ST, G, R])
        lowT = sb("lowT", [4 * R, 2 * ST, P], F32R)
        x1 = sb("x1", [P, 2, ST, D])
        bias_t = sb("bias_t", [P, 2, D])
        mrow = sb("mrow", [P, S])
        s_col = sb("s_col", [P, 2 * ST])
        rowsum = sb("rowsum", [P, 2 * ST])
        zc = sb("zc", [P, 2 * ST])
        rz = sb("rz", [P, 2 * ST])
        d_eia = nc.dram_tensor("d_eia", [E, P, DT * P], F32, kind="Internal").ap()
        d_eib = nc.dram_tensor("d_eib", [E, 2 * R, F], F32, kind="Internal").ap()
        d_eob = nc.dram_tensor("d_eob", [E, 2 * R, D], F32, kind="Internal").ap()

        hbank = [ctx.enter_context(nc.psum_tensor(f"hbank{n}", [P, 512], F32)) for n in range(2)]
        obank = [ctx.enter_context(nc.psum_tensor(f"obank{n}", [P, 512], F32)) for n in range(3)]
        mbank = [ctx.enter_context(nc.psum_tensor(f"mbank{n}", [P, 512], F32)) for n in range(3)]
        H_BANKS = (hbank[0], hbank[1], obank[1], obank[2])
        W2_FROM = 3
        O_OF = (0, 1, 2, 0)
        O_W = (R, 0)
        O_LOW = (0, D)

        WI_BANKS = (obank[2], mbank[0], mbank[1], mbank[2])
        EOA_BANKS = (obank[2], mbank[0])
        WO_BANKS = (obank[0], obank[1], mbank[1], mbank[2])

        STEADY = Places(
            xT=(x1T_h, x1T_l), x1=x1, x2=x2, x1t=(mbank[0], mbank[1]), tt=(mbank[2], mbank[1]),
            parts=(slice(0, N2),), a=(mbank[0],), sr=(mbank[2],),
            pool=(mbank[1], mbank[2], mbank[0], mbank[1]), ut=(mbank[2], mbank[0]), out=(mbank[1], mbank[2]))
        LAST = Places(
            xT=(x0T_h, x0T_l), x1=x0, x2=x1, x1t=(hbank[1], obank[1]), tt=(hbank[0], mbank[2]),
            parts=(slice(0, S), slice(S, N2)), a=(obank[1], obank[0]), sr=(hbank[1], obank[2]),
            pool=(hbank[0], hbank[1], obank[1], obank[0]), ut=(mbank[0], obank[2]), out=(mbank[1], mbank[2]))

        names = """ids_in wi_in cia_in cib_in ewia_in ewib_in wo_in coa_in cob_in ewoa_in ewob_in w2_in0 w2_in1 small_in
            x0_in xres_in0 xres_in1 eia_in eib_in eob_in t_in bias_in out_free eia_saved eib_saved eob_saved
            ident_ok cib_ok ewib_ok cob_ok ewob_ok masks_ok cnt_ok ones_ok small_ok
            pe_eia pe_eib pe_cib pe_wi pe_cob pe_eob pe_eoa pe_wo pe_w2
            act_eia act_eib act_cia act_cib act_wi act_coa act_cob act_eob act_eoa act_wo act_w2
            dve_eia dve_eib dve_cia dve_cib dve_cob dve_coa dve_wi dve_eob dve_eoa dve_wo dve_w2
            pe_h pe_o pe_up pe_lt pe_low pe_x0t pe_x1t pe_tt pe_a pe_sr pe_pool pe_ut
            pe_out
            act_h act_x0t act_low act_lt act_x1t act_x1h act_tt act_tanh act_th act_srow act_exp
            act_ph act_x2h act_ut
            dve_h dve_x0t dve_low dve_lowrep dve_lt dve_x1 dve_x1t dve_tt dve_tstk dve_sc dve_max
            dve_arg dve_z dve_x2 dve_rs dve_ut dve_out
            pool_coa pool_ti pool_x1l pool_eoa p_lo x2_lo p_lo_last x2_lo_last w2_ok""".split()
        s = {n: sem(n) for n in names}

        def rows(t):
            return t.rearrange("(t p) n -> p t n", p=P)

        def sp_stack_in(eng, dst, src, reps, signal):
            eng.dma_start(dst, src.to_broadcast([reps, src.shape[1], src.shape[2]])).then_inc(signal, 16)

        def sp_load(eng, which, i, low, high):
            return [eng.value_load(ids[0:1, which, bass.ds(2 * i + j, 1)], min_val=low, max_val=high)
                    for j in range(2)]

        def sp_eia(eng, es):
            for j, e in enumerate(es):
                eng.dma_start(eia[:, j].rearrange("p k c -> p (k c)").bitcast(F32),
                              d_eia[bass.ds(e, 1)].rearrange("e p n -> (e p) n")).then_inc(s["eia_in"], 16)

        def sp_eib(eng, es):
            for j, e in enumerate(es):
                sp_stack_in(eng, eib[:, j].bitcast(F32), d_eib[bass.ds(e, 1)], 4, s["eib_in"])

        def sp_eob(eng, es):
            for j, e in enumerate(es):
                sp_stack_in(eng, eob[:, j].bitcast(F32), d_eob[bass.ds(e, 1)], 2, s["eob_in"])

        def sp_t(eng, ks):
            for j, k in enumerate(ks):
                eng.dma_start(t_raw[:, j], T[bass.ds(k - 1, 1)].rearrange("e (t p) n -> p (e t) n", p=P)
                              ).then_inc(s["t_in"], 16)

        def sp_bias(eng, es):
            for j, e in enumerate(es):
                eng.dma_start(bias_t[:, j], bias2[bass.ds(e, 1)].to_broadcast([P, D])
                              ).then_inc(s["bias_in"], 16)

        def sp_x(eng, i, dst, j, n, signal):
            eng.dma_start(dst[:, j:j + n].rearrange("p b t d -> p (b t) d"),
                          x[bass.ds(2 * i + j, n)].rearrange("b (t p) d -> p (b t) d", p=P)
                          ).then_inc(signal, 16)

        def sp_body(eng, i, tail):
            here = sp_load(eng, 0, i, 0, E - 1)
            steps = sp_load(eng, 2, i, 1, T.shape[0])
            if tail is not LAST:
                after = sp_load(eng, 0, i + 1, 0, E - 1)
                eng.wait_ge(s["pe_x0t"], 2 * i + 2)
                sp_x(eng, i + 1, x0, 0, 2, s["x0_in"])
                eng.wait_ge(s["pe_low"], i + 1)
                sp_eia(eng, after)
            if tail:
                eng.wait_ge(s["pe_up"], 4 * i)
                sp_eob(eng, here)
                eng.wait_ge(s["pe_tt"], 2 * i)
                eng.wait_ge(s["dve_rs"], 2 * i)
                sp_t(eng, steps)
            if tail is not LAST:
                eng.wait_ge(s["pe_h"], FT * (i + 1))
                sp_eib(eng, after)
            if not tail:
                eng.wait_ge(s["pe_w2"], E)
                eng.wait_ge(s["small_ok"], 4)
                sp_t(eng, steps)
            if tail is STEADY:
                for j in range(2):
                    eng.wait_ge(s["dve_x2"], 4 * i - 2 + 2 * j)
                    sp_x(eng, i, x1, j, 1, s[f"xres_in{j}"])
            if tail:
                sp_out(eng, i - 1, x2)
                sp_bias(eng, here)
            if tail is LAST:
                sp_out(eng, i, x1)

        def sp_out(eng, p, src):
            for j in range(2):
                eng.wait_ge(s["dve_out"], 2 * p + 2 + j)
                eng.dma_start(out[bass.ds(2 * p + j, 1)].rearrange("b (t p) d -> p (b t) d", p=P),
                              src[:, j]).then_inc(s["out_free"], 16)

        def sp_prologue(eng):
            def stacked(dst, src, reps, signal):
                sp_stack_in(eng, dst, src.rearrange("(o r) n -> o r n", o=1), reps, s[signal])

            eng.dma_start(ewia_raw[:], ewi_a.rearrange("e r d -> (e r) d")).then_inc(s["ewia_in"], 16)
            eng.dma_start(cib_raw[:], cwi_b.rearrange("(p t) r -> p (t r)", p=P)).then_inc(s["cib_in"], 16)
            stacked(cia_raw[:], cwi_a, G, "cia_in")
            eng.dma_start(wi_raw[:], rows(wi)).then_inc(s["wi_in"], 16)
            eng.dma_start(ewib_raw[:], ewi_b.rearrange("e (p t) r -> p e (t r)", p=P)).then_inc(s["ewib_in"], 16)
            eng.dma_start(cob_raw[:], cwo_b.rearrange("(p t) r -> p (t r)", p=P)).then_inc(s["cob_in"], 16)
            stacked(coa_raw[:], cwo_a, G, "coa_in")
            for n, t in enumerate((expert_id, mask_id, step_id)):
                eng.dma_start(ids[0:1, n], t.rearrange("(o n) -> o n", o=1)).then_inc(s["ids_in"], 16)
            sp_x(eng, 0, x0, 0, 2, s["x0_in"])
            eng.dma_start(wo_raw[:], rows(wo)).then_inc(s["wo_in"], 16)
            eng.dma_start(ewob_raw[:], ewo_b.rearrange("e (p t) r -> p e (t r)", p=P)).then_inc(s["ewob_in"], 16)
            eng.wait_ge(s["ids_in"], 48)
            first = sp_load(eng, 0, 0, 0, E - 1)
            eng.wait_ge(s["dve_eib"], 2)
            for hl in range(2):
                eng.dma_start(d_eib[:, hl * R:(hl + 1) * R], eib_st[:, hl].bitcast(F32)).then_inc(s["eib_saved"], 16)
            eng.dma_start(ewoa_raw[:], ewo_a.rearrange("e r f -> (e r) f")).then_inc(s["ewoa_in"], 16)
            eng.wait_ge(s["eib_saved"], 32)
            sp_eib(eng, first)

            def w2_half(n):
                eng.dma_start(w2_raw[:, n * E // 2:(n + 1) * E // 2].rearrange("p e t n -> p (e t) n"),
                              W2[n * E // 2:(n + 1) * E // 2].rearrange("e (t p) n -> p (e t) n", p=P)
                              ).then_inc(s[f"w2_in{n}"], 16)

            w2_half(0)
            eng.wait_ge(s["dve_eia"], DT)
            eng.dma_start(d_eia.rearrange("e p n -> p e n"),
                          eia_st[:].rearrange("p e k c -> p e (k c)").bitcast(F32)).then_inc(s["eia_saved"], 16)
            w2_half(1)
            eng.dma_start(w1_raw[:], W1.rearrange("(t p) a -> p t a", p=P)).then_inc(s["small_in"], 16)
            for n in range(2):
                c = slice(n * A, (n + 1) * A)
                eng.dma_start(b1_c[c], b1.rearrange("(a o) -> a o", o=1)).then_inc(s["small_in"], 16)
                eng.dma_start(v_c[c], v.rearrange("(a o) -> a o", o=1)).then_inc(s["small_in"], 16)
            eng.wait_ge(s["dve_eob"], 1)
            for hl in range(2):
                eng.dma_start(d_eob[:, hl * R:(hl + 1) * R], eob_st[:, hl].bitcast(F32)).then_inc(s["eob_saved"], 16)
            eng.wait_ge(s["eob_saved"], 32)
            sp_eob(eng, first)
            for j in range(2):
                sp_x(eng, 0, x1, j, 1, s[f"xres_in{j}"])
            sp_bias(eng, first)
            eng.wait_ge(s["eia_saved"], 16)
            eng.sem_inc(s["out_free"], 32)

        def split3(eng, dst, lhs, rhs, first, last):
            (lh, ll), (rh, rl) = lhs, rhs
            eng.matmul(dst, lh, rh, start=first, stop=False, skip_group_check=True)
            eng.matmul(dst, lh, rl, start=False, stop=False, skip_group_check=True)
            return eng.matmul(dst, ll, rh, start=False, stop=last, skip_group_check=True)

        def pe_x0t(eng, i, j):
            for k in range(DT):
                for t in range(ST):
                    at = k * S + t * P
                    m = eng.transpose(hbank[1 - j][:, at:at + P], x0[:, j, t, k * P:(k + 1) * P], ident[:])
            m.then_inc(s["pe_x0t"], 1)

        def pe_low(eng, i):
            eng.wait_ge(s["eia_in"], 32 * (i + 1))
            eng.wait_ge(s["dve_x0t"], 2 * (i + 1))
            for j in range(2):
                c = slice(j * S, (j + 1) * S)
                for k in range(DT):
                    eng.matmul(hbank[1][:, c], eia[:, j, k], x0T_h[:, k, c], start=k == 0 and j == 0,
                               stop=False, skip_group_check=True)
                    m = eng.matmul(hbank[1][:, c], eia[:, j, k], x0T_l[:, k, c], start=False,
                                   stop=k == DT - 1, skip_group_check=True)
            m.then_inc(s["pe_low"], 1)

        def pe_h(eng, i, f, tail):
            if f == 1:
                eng.wait_ge(s["dve_low"], i + 1)
            if f == 2:
                eng.wait_ge(s["dve_wo"], FT // 2)
                eng.wait_ge(s["dve_eoa"], 2)
            if f >= 4:
                eng.wait_ge(s["dve_h"], FT * i + f - 3)
            h = H_BANKS[f % 4]
            c = slice(f * P, (f + 1) * P)
            for k in range(DT):
                split3(eng, h[:, :], (wiT_h[:, k, c], wiT_l[:, k, c]), (x0T_h[:, k], x0T_l[:, k]),
                       k == 0, False)
            if f == 0:
                if tail:
                    pe_x1t(eng, i - 1, 0, STEADY)
                eng.wait_ge(s["eib_in"], 32 * (i + 1))
                eng.wait_ge(s["dve_low"], i + 1)
            for j in range(2):
                q = slice(j * S, (j + 1) * S)
                m = eng.matmul(h[:, q], eib[:, j, c], low[:, q], start=False, stop=j == 1,
                               skip_group_check=True)
            m.then_inc(s["pe_h"], 1)

        def pe_o(eng, i, n, fs=range(FT)):
            j, t = divmod(n, ST)
            if n in (0, 2) and fs[0] == 0:
                eng.wait_ge(s["pool_eoa"], 4 * i + 2 + n)
            if n == 3 and fs[0] == 0:
                eng.wait_ge(s["dve_x1"], 4 * i + 1)
            o = obank[O_OF[n]]
            c0 = j * R
            for f in fs:
                if n == 0 and f in (0, FT - 2, FT - 1):
                    eng.wait_ge(s["dve_h"], FT * i + max(f + 1, FT - 2))
                q = slice(j * S + t * P, j * S + (t + 1) * P)
                m = split3(eng, o[:, 0:R + D], (hT_h[:, f, q], hT_l[:, f, q]),
                           (woT_h[:, f, c0:c0 + R + D], woT_l[:, f, c0:c0 + R + D]), f == 0, False)
            if fs[-1] == FT - 1:
                m.then_inc(s["pe_o"], 1)

        def pe_lt(eng, i, j, nxt):
            eng.wait_ge(s["dve_lowrep"], 4 * i + 2 * j + 2)
            if j and nxt:
                eng.wait_ge(s["dve_x0t"], 2 * (i + 2))
            for t in range(ST):
                m = eng.transpose(hbank[0][:, t * P:(t + 1) * P],
                                  low_o[:, j * ST + t].rearrange("p a r -> p (a r)"), ident[:])
            m.then_inc(s["pe_lt"], 1)

        def pe_up(eng, i, j):
            if j == 0:
                eng.wait_ge(s["eob_in"], 32 * (i + 1))
            eng.wait_ge(s["dve_lt"], 2 * i + j + 1)
            for t in range(ST):
                n = j * ST + t
                w = O_W[j]
                eng.matmul(obank[O_OF[n]][:, w:w + D], lowT[:, n], eob[:, j], start=False, stop=True,
                           skip_group_check=True).then_inc(s["pe_up"], 1)

        def pe_x1t(eng, p, j, at):
            if at is LAST:
                eng.wait_ge(s["dve_x1"], 4 * p + 2 + 2 * j)
            elif j == 0:
                eng.wait_ge(s["dve_x1"], 4 * p + 4)
            else:
                eng.wait_ge(s["dve_w2"], E)
            for k in range(DT):
                for t in range(ST):
                    c = k * S + t * P
                    m = eng.transpose(at.x1t[j][:, c:c + P], at.x1[:, j, t, k * P:(k + 1) * P], ident[:])
            m.then_inc(s["pe_x1t"], 1)

        def pe_tt(eng, p, j, at):
            if j == 0:
                eng.wait_ge(s["pool_ti"], 4 * p + 4)
            if j == 0 and at is STEADY:
                eng.wait_ge(s["dve_out"], 2 * p + 1)
            for k in range(ST):
                for t in range(ST):
                    c = k * S + t * P
                    m = eng.transpose(at.tt[j][:, c:c + P], t_raw[:, j, t, k * P:(k + 1) * P], ident[:])
            m.then_inc(s["pe_tt"], 1)

        def pe_a(eng, p, m, at):
            eng.wait_ge(s["dve_x1t"], 2 * p + 2 if at is STEADY else 2 * p + 1 + m)
            c = at.parts[m]
            xh, xl = at.xT
            for k in range(DT):
                mm = split3(eng, at.a[m][:, 0:c.stop - c.start], (w1_h[:, k], w1_l[:, k]),
                            (xh[:, k, c], xl[:, k, c]), k == 0, k == DT - 1)
            mm.then_inc(s["pe_a"], 1)

        def pe_scores(eng, p, m, at):
            eng.wait_ge(s["dve_tstk"], p + 1 + m)
            if at is STEADY:
                eng.wait_ge(s["dve_tt"], 2 * p + 1)
            c = at.parts[m]
            bank = at.sr[m][:, 0:c.stop - c.start]
            eng.matmul(bank, v_h[:], tstk[:, c], start=True, stop=False)
            eng.matmul(bank, v_l[:], tstk[:, c], start=False, stop=True).then_inc(s["pe_sr"], 1)

        def pe_pool(eng, p, j, at):
            if j == 0 and at is STEADY:
                eng.wait_ge(s["dve_tt"], 2 * p + 2)
                eng.wait_ge(s["act_srow"], p + 1)
            eng.wait_ge(s["act_x1h"], 2 * p + 1 + j)
            eng.wait_ge(s["pool_x1l"], 2 * p + 1 + j)
            if at is LAST and j:
                eng.wait_ge(s["p_lo_last"], 1)
            else:
                eng.wait_ge(s["p_lo"], 2 * p + 1 + j)
            for t in range(ST):
                bank = at.pool[ST * j + t]
                if j and t and at is STEADY:
                    eng.wait_ge(s["dve_x2"], 4 * p + 1)
                c = slice(t * P, (t + 1) * P)
                for l in range(ST):
                    m = split3(eng, bank[:, 0:D + 2], (p_h[:, j, l, c], p_l[:, j, l, c]),
                               (x1_h[:, j, l], x1_l[:, j, l]), l == 0, l == ST - 1)
                m.then_inc(s["pe_pool"], 1)

        def wait_x2_lo(eng, p, j, at):
            if at is LAST:
                eng.wait_ge(s["x2_lo_last"], j + 1)
            else:
                eng.wait_ge(s["x2_lo"], 2 * p + 1 + j)

        def pe_ut(eng, p, j, at):
            wait_x2_lo(eng, p, j, at)
            eng.wait_ge(s["dve_tt"], 2 * p + 2)
            for d in range(DT):
                c = slice(d * P, (d + 1) * P)
                for k in range(ST):
                    m = split3(eng, at.ut[j][:, d * S:(d + 1) * S], (x2_h[:, j, k, c], x2_l[:, j, k, c]),
                               (tT_h[:, j, k], tT_l[:, j, k]), k == 0 and d == 0, k == ST - 1)
            m.then_inc(s["pe_ut"], 1)

        def pe_expert(eng, p, j):
            return eng.value_load(ids[0:1, 0, bass.ds(2 * p + j, 1)], min_val=0, max_val=E - 1)

        def pe_out(eng, p, j, t, e, at):
            if t == 0:
                eng.wait_ge(s["dve_ut"], 2 * p + 1 + j)
            if j == 0 and t == 0:
                eng.wait_ge(s["dve_x2"], 4 * p + 4 if at is STEADY else 4 * p + 2)
            wh = w2T_h[:, bass.ds(e, 1)].rearrange("p e k n -> p (e k) n")
            wl = w2T_l[:, bass.ds(e, 1)].rearrange("p e k n -> p (e k) n")
            c = slice(j * S + t * P, j * S + (t + 1) * P)
            uh, ul = at.xT
            for k in range(DT):
                m = split3(eng, at.out[j][:, t * D:(t + 1) * D], (uh[:, k, c], ul[:, k, c]),
                           (wh[:, k], wl[:, k]), k == 0 and t == 0, k == DT - 1)
            m.then_inc(s["pe_out"], 1)

        def pe_w2_prep(eng, e):
            eng.wait_ge(s["w2_ok"], e + 1)
            if e >= 3:
                eng.wait_ge(s["dve_w2"], e - 2)
            for k in range(DT):
                for t in range(DT):
                    at = k * D + t * P
                    m = eng.transpose(mbank[e % 3][:, at:at + P], w2_raw[:, e, t, k * P:(k + 1) * P], ident[:])
            m.then_inc(s["pe_w2"], 1)

        def pe_body(eng, i, tail):
            p = i - 1
            first = not tail
            for f in range(FT):
                pe_h(eng, i, f, tail)
                if first and f >= W2_FROM:
                    pe_w2_prep(eng, f - W2_FROM)
                if tail and f == 0:
                    pe_x1t(eng, p, 1, STEADY)
                if tail and f == 1:
                    pe_tt(eng, p, 0, STEADY)
                    pe_a(eng, p, 0, STEADY)
                if tail and f == 2:
                    pe_tt(eng, p, 1, STEADY)
                if tail and f == 3:
                    pe_scores(eng, p, 0, STEADY)
            pe_o(eng, i, 0)
            if tail is LAST:
                pe_last(eng)
                return
            if first:
                pe_w2_prep(eng, E - 3)
            if tail:
                pe_pool(eng, p, 0, STEADY)
            pe_o(eng, i, 1)
            if first:
                pe_w2_prep(eng, E - 2)
            if tail:
                pe_pool(eng, p, 1, STEADY)
            if tail:
                pe_ut(eng, p, 0, STEADY)
            pe_lt(eng, i, 0, True)
            pe_o(eng, i, 2)
            pe_up(eng, i, 0)
            if tail:
                pe_ut(eng, p, 1, STEADY)
                e0 = pe_expert(eng, p, 0)
                pe_out(eng, p, 0, 0, e0, STEADY)
                pe_out(eng, p, 0, 1, e0, STEADY)
            eng.wait_ge(s["x0_in"], 16 * (i + 2))
            pe_x0t(eng, i + 1, 0)
            eng.wait_ge(s["dve_lt"], 2 * i + 1)
            pe_x0t(eng, i + 1, 1)
            pe_o(eng, i, 3)
            if tail:
                e1 = pe_expert(eng, p, 1)
                pe_out(eng, p, 1, 0, e1, STEADY)
            else:
                pe_w2_prep(eng, E - 1)
            pe_lt(eng, i, 1, True)
            if tail:
                pe_out(eng, p, 1, 1, e1, STEADY)
            pe_low(eng, i + 1)
            pe_up(eng, i, 1)

        def pe_last(eng):
            q = PAIRS - 1
            p = q - 1
            pe_o(eng, q, 1)
            pe_o(eng, q, 2, range(2))
            pe_lt(eng, q, 0, False)
            pe_o(eng, q, 2, range(2, 6))
            pe_up(eng, q, 0)
            pe_o(eng, q, 2, range(6, FT))
            pe_o(eng, q, 3, range(FT // 2))
            pe_x1t(eng, q, 0, LAST)
            pe_o(eng, q, 3, range(FT // 2, FT))
            e = [pe_expert(eng, p, j) for j in range(2)]
            pe_a(eng, q, 0, LAST)
            pe_lt(eng, q, 1, False)
            pe_pool(eng, p, 0, STEADY)
            pe_up(eng, q, 1)
            pe_scores(eng, q, 0, LAST)
            eng.wait_ge(s["act_tanh"], q + 1)
            pe_x1t(eng, q, 1, LAST)
            pe_pool(eng, p, 1, STEADY)
            pe_a(eng, q, 1, LAST)
            pe_ut(eng, p, 0, STEADY)
            pe_scores(eng, q, 1, LAST)
            pe_ut(eng, p, 1, STEADY)
            pe_tt(eng, q, 0, LAST)
            eng.wait_ge(s["dve_ut"], 2 * p + 1)
            pe_tt(eng, q, 1, LAST)
            pe_out(eng, p, 0, 0, e[0], STEADY)
            pe_out(eng, p, 0, 1, e[0], STEADY)
            eng.wait_ge(s["dve_tt"], 2 * q + 2)
            eng.wait_ge(s["act_srow"], q + 1)
            pe_pool(eng, q, 0, LAST)
            e += [pe_expert(eng, q, j) for j in range(2)]
            pe_pool(eng, q, 1, LAST)
            pe_out(eng, p, 1, 0, e[1], STEADY)
            pe_out(eng, p, 1, 1, e[1], STEADY)
            pe_ut(eng, q, 0, LAST)
            eng.wait_ge(s["act_srow"], q + 2)
            pe_ut(eng, q, 1, LAST)
            eng.wait_ge(s["dve_out"], 2 * p + 2)
            pe_out(eng, q, 0, 0, e[2], LAST)
            pe_out(eng, q, 0, 1, e[2], LAST)
            eng.wait_ge(s["dve_out"], 2 * p + 3)
            pe_out(eng, q, 1, 0, e[3], LAST)
            pe_out(eng, q, 1, 1, e[3], LAST)

        def pe_warm(eng, bank, n):
            for _ in range(n):
                eng.transpose(bank[:, 0:P], ident[:], ident[:])

        def pe_prologue(eng):
            eng.wait_ge(s["ident_ok"], 2)
            pe_warm(eng, mbank[2], 8)
            eng.wait_ge(s["ewia_in"], 16)
            for k in range(DT):
                m = eng.transpose(mbank[0][:, k * P:(k + 1) * P], ewia_raw[:, k * P:(k + 1) * P], ident[:])
            m.then_inc(s["pe_eia"], 1)
            eng.wait_ge(s["cib_ok"], 1)
            for t in range(FT):
                m = eng.transpose(obank[t // 4][:, (t % 4) * P:(t % 4 + 1) * P], cib_s[:, t], ident[:])
                if t % 4 == 3:
                    m.then_inc(s["pe_cib"], 1)
            pe_warm(eng, mbank[2], 12)
            eng.wait_ge(s["wi_in"], 16)
            eng.wait_ge(s["dve_cia"], 1)
            eng.wait_ge(s["dve_cib"], 2)
            for n, bank in enumerate(WI_BANKS):
                k, a = divmod(n, 2)
                if n == 1:
                    eng.wait_ge(s["dve_eia"], DT)
                eng.matmul(bank[:, :], cia_st[:, k * P:(k + 1) * P], cibT[:, a * 512:(a + 1) * 512],
                           start=True, stop=False, skip_group_check=True)
                for t in range(4):
                    m = eng.matmul(bank[:, t * P:(t + 1) * P], wi_raw[:, 4 * a + t, k * P:(k + 1) * P],
                                   ident[:], start=False, stop=True, skip_group_check=True)
                m.then_inc(s["pe_wi"], 1)
                if n == 1:
                    eng.wait_ge(s["ewib_ok"], 1)
                    for t in range(FT):
                        m = eng.transpose(hbank[t // 4][:, (t % 4) * P:(t % 4 + 1) * P],
                                          ewib_s[:, t], ident[:])
                        if t % 4 == 3:
                            m.then_inc(s["pe_eib"], 1)
                    eng.wait_ge(s["cob_ok"], 1)
                    for t in range(DT):
                        m = eng.transpose(obank[0][:, t * P:(t + 1) * P], cob_s[:, t], ident[:])
                    m.then_inc(s["pe_cob"], 1)
            eng.wait_ge(s["x0_in"], 16)
            eng.wait_ge(s["dve_eib"], 2)
            pe_x0t(eng, 0, 0)
            pe_x0t(eng, 0, 1)
            eng.wait_ge(s["wo_in"], 16)
            eng.wait_ge(s["pool_coa"], 1)
            eng.wait_ge(s["dve_coa"], 1)
            eng.wait_ge(s["dve_cob"], 1)
            for n, bank in enumerate(WO_BANKS):
                if n == 2:
                    eng.wait_ge(s["dve_wi"], 4)
                for a in range(2):
                    f = 2 * n + a
                    eng.matmul(bank[:, a * D:(a + 1) * D], coa_st[:, f * P:(f + 1) * P], cobT[:],
                               start=a == 0, stop=False, skip_group_check=True)
                    for t in range(DT):
                        at = a * D + t * P
                        m = eng.matmul(bank[:, at:at + P], wo_raw[:, t, f * P:(f + 1) * P], ident[:],
                                       start=False, stop=True, skip_group_check=True)
                m.then_inc(s["pe_wo"], 1)
            pe_low(eng, 0)
            eng.wait_ge(s["ewob_ok"], 1)
            eng.wait_ge(s["dve_wo"], 1)
            for t in range(DT):
                m = eng.transpose(obank[0][:, t * P:(t + 1) * P], ewob_s[:, t], ident[:])
            m.then_inc(s["pe_eob"], 1)
            eng.wait_ge(s["ewoa_in"], 16)
            for a, bank in enumerate(EOA_BANKS):
                for t in range(4):
                    f = 4 * a + t
                    m = eng.transpose(bank[:, t * P:(t + 1) * P], ewoa_raw[:, f * P:(f + 1) * P], ident[:])
                m.then_inc(s["pe_eoa"], 1)
            eng.wait_ge(s["ids_in"], 48)

        def act_x0t(eng, i, j):
            eng.wait_ge(s["pe_x0t"], 2 * i + j + 1)
            nc.scalar.copy(x0T_h[:, :, j * S:(j + 1) * S],
                           hbank[1 - j][:, :].rearrange("p (k n) -> p k n", k=DT)).then_inc(s["act_x0t"], 1)

        def act_steps(eng, i, p, at):
            copy = nc.scalar.copy
            xh = at.xT[0]

            def h(f):
                eng.wait_ge(s["pe_h"], FT * i + f + 1)
                nc.scalar.activation(hT_h[:, f], H_BANKS[f % 4][:, :], ACT.Relu).then_inc(s["act_h"], 1)

            def lt(j):
                eng.wait_ge(s["pe_lt"], 2 * i + j + 1)
                copy(lowT[:, j * ST:(j + 1) * ST],
                     hbank[0][0:4 * R, 0:S].rearrange("p (t n) -> p t n", t=ST)).then_inc(s["act_lt"], 1)

            def x1t(j):
                eng.wait_ge(s["pe_x1t"], 2 * p + j + 1)
                copy(xh[:, :, j * S:(j + 1) * S],
                     at.x1t[j][:, :].rearrange("p (k n) -> p k n", k=DT)).then_inc(s["act_x1t"], 1)

            def x1h(j):
                copy(x1_h[:, j, :, 0:D], at.x1[:, j]).then_inc(s["act_x1h"], 1)

            def tt(j):
                eng.wait_ge(s["pe_tt"], 2 * p + 1 + j)
                copy(tT_h[:, j], at.tt[j][:, :].rearrange("p (k n) -> p k n", k=ST)).then_inc(s["act_tt"], 1)

            def tanh(m):
                c = at.parts[m]
                eng.wait_ge(s["pe_a"], p + 1 + m)
                nc.scalar.activation(th[:, c], at.a[m][:, 0:c.stop - c.start], ACT.Tanh, bias=b1_c[:]
                                     ).then_inc(s["act_tanh"], 1)
                eng.wait_ge(s["act_tanh"], p + 1 + m)
                copy(tstk[:, c], th[:, c]).then_inc(s["act_th"], 1)

            def srow(m):
                c = at.parts[m]
                eng.wait_ge(s["pe_sr"], p + 1 + m)
                copy(th[:, c], at.sr[m][:, 0:c.stop - c.start]).then_inc(s["act_srow"], 1)

            def exp(j):
                eng.wait_ge(s["dve_arg"], 4 * p + 2 * j + 2)
                nc.scalar.activation(terms[:, j], terms[:, j], ACT.Exp, scale=-1.0).then_inc(s["act_exp"], 1)
                eng.wait_ge(s["act_exp"], 2 * p + j + 1)
                copy(p_h[:, j], terms[:, j]).then_inc(s["act_ph"], 1)

            def x2h(j):
                eng.wait_ge(s["dve_x2"], 4 * p + 2 * j + 2)
                copy(x2_h[:, j], at.x2[:, j]).then_inc(s["act_x2h"], 1)

            def ut(j):
                eng.wait_ge(s["pe_ut"], 2 * p + j + 1)
                copy(xh[:, :, j * S:(j + 1) * S],
                     at.ut[j][:, :].rearrange("p (k n) -> p k n", k=DT)).then_inc(s["act_ut"], 1)

            def w2(e):
                eng.wait_ge(s["pe_w2"], e + 1)
                copy(w2T_h[:, e], mbank[e % 3][:, :].rearrange("p (k n) -> p k n", k=DT)
                     ).then_inc(s["act_w2"], 1)

            do = Steps()
            do.h, do.lt, do.x1t = h, lt, x1t
            do.x1h, do.tt, do.tanh = x1h, tt, tanh
            do.srow, do.exp, do.x2h = srow, exp, x2h
            do.ut, do.w2 = ut, w2
            return do

        def act_body(eng, i, tail):
            do = act_steps(eng, i, i - 1, STEADY)
            if not tail:
                for f in range(FT):
                    do.h(f)
                    if f >= W2_FROM:
                        do.w2(f - W2_FROM)
                for e in range(FT - W2_FROM, E - 1):
                    do.w2(e)
                eng.wait_ge(s["small_in"], 80)
            else:
                do.x1t(0)
                do.x1t(1)
                do.h(0)
                do.h(1)
                do.tt(0)
                do.tanh(0)
                do.h(2)
                do.tt(1)
                do.x1h(0)
                do.h(3)
                do.srow(0)
                do.x1h(1)
                for f in range(4, 7):
                    do.h(f)
                do.exp(0)
                do.h(7)
                do.exp(1)
            if tail is LAST:
                act_last(eng, do)
                return
            if tail:
                do.x2h(0)
                do.x2h(1)
            if tail:
                do.ut(0)
            do.lt(0)
            if tail:
                do.ut(1)
            act_x0t(eng, i + 1, 0)
            act_x0t(eng, i + 1, 1)
            do.lt(1)
            if not tail:
                do.w2(E - 1)
            eng.wait_ge(s["pe_low"], i + 2)
            nc.scalar.copy(low[:], hbank[1][:, :]).then_inc(s["act_low"], 1)

        def act_last(eng, do):
            last = act_steps(eng, PAIRS - 1, PAIRS - 1, LAST)
            last.lt(0)
            last.x1t(0)
            last.tanh(0)
            last.lt(1)
            last.srow(0)
            last.x1t(1)
            do.x2h(0)
            last.x1h(0)
            last.tanh(1)
            do.x2h(1)
            do.ut(0)
            last.srow(1)
            last.x1h(1)
            last.exp(0)
            do.ut(1)
            last.tt(0)
            last.tt(1)
            last.exp(1)
            last.x2h(0)
            last.x2h(1)
            last.ut(0)
            last.ut(1)

        def act_prologue(eng):
            copy, mul = nc.scalar.copy, nc.scalar.mul
            eng.wait_ge(s["pe_eia"], 1)
            for k in range(DT):
                src = mbank[0][:, k * P:(k + 1) * P].rearrange("p (e o r) -> p e o r", e=E, o=1)
                for c in (0, 4 * R):
                    m = copy(eia_st[:, :, k, c:c + 2 * R].rearrange("p e (g r) -> p e g r", g=2),
                             src.to_broadcast([P, E, 2, R]))
                m.then_inc(s["act_eia"], 1)
            eng.wait_ge(s["cia_in"], 16)
            copy(cia_st[:], cia_raw[:]).then_inc(s["act_cia"], 1)
            for a in range(2):
                eng.wait_ge(s["pe_cib"], 1 + a)
                dst = cibT[:].rearrange("r (n t) -> r t n", t=FT)
                copy(dst[:, 4 * a:4 * a + 4], obank[a][:, :].rearrange("r (t n) -> r t n", t=4)
                     ).then_inc(s["act_cib"], 1)
            for n, bank in enumerate(WI_BANKS):
                k, a = divmod(n, 2)
                eng.wait_ge(s["pe_wi"], 1 + n)
                copy(wiT_h[:, k, a * 512:(a + 1) * 512], bank[:, :]).then_inc(s["act_wi"], 1)
                if n == 1:
                    eng.wait_ge(s["coa_in"], 16)
                    copy(coa_st[:], coa_raw[:]).then_inc(s["act_coa"], 1)
                    for a in range(2):
                        eng.wait_ge(s["pe_eib"], 1 + a)
                        dst = eib_st[:, 0].rearrange("p (n t) -> p t n", t=FT)
                        mul(dst[:, 4 * a:4 * a + 4], hbank[a][:, :].rearrange("p (t n) -> p t n", t=4),
                            ALPHA).then_inc(s["act_eib"], 1)
                    eng.wait_ge(s["pe_cob"], 1)
                    copy(cobT[:].rearrange("r (n t) -> r t n", t=DT),
                         obank[0][:, 0:D].rearrange("r (t n) -> r t n", t=DT)).then_inc(s["act_cob"], 1)
            act_x0t(eng, 0, 0)
            act_x0t(eng, 0, 1)
            for n, bank in enumerate(WO_BANKS):
                eng.wait_ge(s["pe_wo"], 1 + n)
                copy(woT_h[:, 2 * n:2 * n + 2, R:R + D], bank[:, :].rearrange("p (a n) -> p a n", a=2)
                     ).then_inc(s["act_wo"], 1)
            eng.wait_ge(s["pe_low"], 1)
            copy(low[:], hbank[1][:, :]).then_inc(s["act_low"], 1)
            eng.wait_ge(s["pe_eob"], 1)
            mul(eob_st[:, 0].rearrange("p (n t) -> p t n", t=DT),
                obank[0][:, 0:D].rearrange("p (t n) -> p t n", t=DT), ALPHA).then_inc(s["act_eob"], 1)
            for a, bank in enumerate(EOA_BANKS):
                eng.wait_ge(s["pe_eoa"], 1 + a)
                copy(ewoT_h[:, 4 * a:4 * a + 4], bank[:, :].rearrange("p (t n) -> p t n", t=4)
                     ).then_inc(s["act_eoa"], 1)

        def minus(dst, src, hi):
            return nc.vector.tensor_tensor(dst, src, hi.bitcast(F32), ALU.subtract)

        def lo_T(lo, hi, bank, j):
            c = slice(j * S, (j + 1) * S)
            return minus(lo[:, :, c], bank[:, :].rearrange("p (k n) -> p k n", k=DT), hi[:, :, c])

        def dve_x0t(eng, i, j):
            eng.wait_ge(s["act_x0t"], 2 * i + j + 1)
            lo_T(x0T_l, x0T_h, hbank[1 - j], j).then_inc(s["dve_x0t"], 1)

        def dve_steps(eng, i, p, at):
            xh, xl = at.xT

            def d_h(f):
                eng.wait_ge(s["act_h"], FT * i + f + 1)
                nc.vector.scalar_tensor_tensor(
                    out=hT_l[:, f], in0=H_BANKS[f % 4][:, :], scalar=0.0, in1=hT_h[:, f].bitcast(F32),
                    op0=ALU.max, op1=ALU.subtract).then_inc(s["dve_h"], 1)

            def d_x1t(j):
                eng.wait_ge(s["act_x1t"], 2 * p + j + 1)
                lo_T(xl, xh, at.x1t[j], j).then_inc(s["dve_x1t"], 1)

            def d_tt(j):
                eng.wait_ge(s["act_tt"], 2 * p + j + 1)
                minus(tT_l[:, j], at.tt[j][:, :].rearrange("p (k n) -> p k n", k=ST),
                      tT_h[:, j]).then_inc(s["dve_tt"], 1)

            def d_lowrep(n):
                j = n // ST
                eng.wait_ge(s["pe_o"], 4 * i + n + 1)
                src = obank[O_OF[n]][:, O_LOW[j]:O_LOW[j] + R].rearrange("p (o r) -> p o r", o=1)
                nc.vector.tensor_copy(low_o[:, n], src.to_broadcast([P, G, R])).then_inc(s["dve_lowrep"], 1)

            def d_lt(j):
                eng.wait_ge(s["act_lt"], 2 * i + j + 1)
                q = slice(2 * R, 4 * R)
                minus(lowT[q, j * ST:(j + 1) * ST], hbank[0][q, 0:S].rearrange("p (t n) -> p t n", t=ST),
                      lowT[q, j * ST:(j + 1) * ST]).then_inc(s["dve_lt"], 1)

            def d_x1(n):
                j, t = divmod(n, ST)
                eng.wait_ge(s["pe_up"], 4 * i + n + 1)
                if at is LAST:
                    eng.wait_ge(s["x0_in"], 16 * (i + 1))
                elif t == 0:
                    eng.wait_ge(s[f"xres_in{j}"], 16 * (i + 1))
                nc.vector.tensor_tensor(at.x1[:, j, t], obank[O_OF[n]][:, O_W[j]:O_W[j] + D], at.x1[:, j, t],
                                        ALU.add).then_inc(s["dve_x1"], 1)

            def d_tstk(m):
                eng.wait_ge(s["act_th"], p + 1 + m)
                q, c = slice(A, P), at.parts[m]
                minus(tstk[q, c], th[q, c], tstk[q, c]).then_inc(s["dve_tstk"], 1)

            def d_pre(j):
                if j == 0 or at is LAST:
                    eng.wait_ge(s["act_srow"], p + 1 + j)
                if j:
                    eng.wait_ge(s["dve_max"], 6 * p + 3)
                row = th[:, j * S:(j + 1) * S]
                nc.vector.tensor_tensor_scan(pre_max[:, S + 1:], row, row, -BIG, ALU.max,
                                             ALU.max).then_inc(s["dve_max"], 1)

            def d_suf(j):
                row = th[:, (j + 1) * S - 1:j * S - 1:-1] if j else th[:, S - 1::-1]
                nc.vector.tensor_tensor_scan(suf_max[:, S - 1::-1], row, row, -BIG, ALU.max,
                                             ALU.max).then_inc(s["dve_max"], 1)

            def d_score_cols(j):
                for l in range(ST):
                    n = ST * j + l
                    nc.vector.tensor_tensor_reduce(
                        out=terms[:, j, l, 0:P], in0=th[:, n * P:(n + 1) * P], in1=ident[:], scale=1.0,
                        scalar=0.0, op0=ALU.mult, op1=ALU.add, accum_out=s_col[:, n:n + 1]
                    ).then_inc(s["dve_sc"], 1)

            def d_kind(j):
                kind = eng.value_load(ids[0:1, 1, bass.ds(2 * p + j, 1)], min_val=0, max_val=2)
                a = eng.value_load(pre_at[0:1, bass.ds(kind, 1)], min_val=0, max_val=S + 1)
                b = eng.value_load(suf_at[0:1, bass.ds(kind, 1)], min_val=0, max_val=S + 1)
                return kind, a, b

            def d_arg(j, where):
                kind, a, b = where
                eng.wait_ge(s["dve_max"], 6 * p + 3 * j + 2)
                if j:
                    eng.wait_ge(s["dve_arg"], 4 * p + 2)
                nc.vector.tensor_tensor(mrow[:], pre_max[:, bass.ds(a, S)], suf_max[:, bass.ds(b, S)],
                                        ALU.max).then_inc(s["dve_max"], 1)
                eng.wait_ge(s["dve_sc"], 4 * p + 2 * j + 2)
                eng.wait_ge(s["dve_max"], 6 * p + 3 * j + 3)
                for l in range(ST):
                    mask = mask_big[:, bass.ds(kind, 1), l].rearrange("p o n -> p (o n)")
                    nc.vector.scalar_tensor_tensor(
                        out=terms[:, j, l], in0=mrow[:], scalar=s_col[:, ST * j + l:ST * j + l + 1], in1=mask,
                        op0=ALU.subtract, op1=ALU.max).then_inc(s["dve_arg"], 1)

            def d_x2(j, where):
                kind = where[0]
                tiles = [(t, ST * j + t, at.pool[ST * j + t]) for t in range(ST)]
                for t, n, bank in tiles:
                    eng.wait_ge(s["pe_pool"], 4 * p + n + 1)
                    nc.vector.tensor_tensor(zc[:, n:n + 1], bank[:, D:D + 1], cnt[:, bass.ds(kind, 1), t],
                                            ALU.mult).then_inc(s["dve_z"], 1)
                c = slice(ST * j, ST * (j + 1))
                eng.wait_ge(s["dve_z"], 6 * p + 3 * j + 2)
                nc.vector.reciprocal(rz[:, c], zc[:, c]).then_inc(s["dve_z"], 1)
                if j == 0 and at is STEADY:
                    eng.wait_ge(s["out_free"], 32 * p + 32)
                eng.wait_ge(s["dve_z"], 6 * p + 3 * j + 3)
                for t, n, bank in tiles:
                    nc.vector.scalar_tensor_tensor(
                        out=at.x2[:, j, t], in0=bank[:, 0:D], scalar=rz[:, n:n + 1], in1=at.x1[:, j, t],
                        op0=ALU.mult, op1=ALU.add).then_inc(s["dve_x2"], 1)

            def d_p_lo(j):
                eng.wait_ge(s["act_ph"], 2 * p + j + 1)
                minus(p_l[:, j], terms[:, j], p_h[:, j]).then_inc(s["p_lo_last"], 1)

            def d_x2_lo(j):
                eng.wait_ge(s["act_x2h"], 2 * p + j + 1)
                minus(x2_l[:, j], at.x2[:, j], x2_h[:, j]).then_inc(s["x2_lo_last"], 1)

            def d_rowsum(j):
                if at is LAST:
                    eng.wait_ge(s["dve_out"], 2 * p + 1)
                eng.wait_ge(s["pool_ti"], 4 * p + 2 * j + 2)
                nc.vector.tensor_reduce(rowsum[:, ST * j:ST * (j + 1)], t_raw[:, j], AX.X, ALU.add
                                        ).then_inc(s["dve_rs"], 1)

            def d_ut(j):
                eng.wait_ge(s["act_ut"], 2 * p + j + 1)
                lo_T(xl, xh, at.ut[j], j).then_inc(s["dve_ut"], 1)

            def d_out(j):
                eng.wait_ge(s["pe_out"], 4 * p + 2 * j + 2)
                wait_x2_lo(eng, p, j, at)
                if j == 0:
                    eng.wait_ge(s["bias_in"], 32 * (p + 1))
                    eng.wait_ge(s["dve_rs"], 2 * p + 2)
                for t in range(ST):
                    m = nc.vector.scalar_tensor_tensor(
                        out=at.x2[:, j, t], in0=bias_t[:, j], scalar=rowsum[:, ST * j + t:ST * j + t + 1],
                        in1=at.out[j][:, t * D:(t + 1) * D], op0=ALU.mult, op1=ALU.add)
                m.then_inc(s["dve_out"], 1)

            def d_w2(e):
                eng.wait_ge(s["act_w2"], e + 1)
                minus(w2T_l[:, e], mbank[e % 3][:, :].rearrange("p (k n) -> p k n", k=DT),
                      w2T_h[:, e]).then_inc(s["dve_w2"], 1)

            do = Steps()
            do.h, do.x1t, do.tt = d_h, d_x1t, d_tt
            do.lowrep, do.lt, do.x1 = d_lowrep, d_lt, d_x1
            do.tstk, do.pre, do.suf = d_tstk, d_pre, d_suf
            do.score_cols, do.kind, do.arg = d_score_cols, d_kind, d_arg
            do.x2, do.p_lo, do.x2_lo = d_x2, d_p_lo, d_x2_lo
            do.rowsum, do.ut, do.out = d_rowsum, d_ut, d_out
            do.w2 = d_w2
            return do

        def dve_body(eng, i, tail):
            do = dve_steps(eng, i, i - 1, STEADY)
            if not tail:
                for f in range(FT):
                    do.h(f)
                    if f >= W2_FROM:
                        do.w2(f - W2_FROM)
                dve_tables()
                do.w2(E - 3)
            else:
                do.x1t(0)
                do.x1t(1)
                do.h(0)
                do.h(1)
                do.tt(0)
                at0 = do.kind(0)
                do.tstk(0)
                do.h(2)
                do.tt(1)
                at1 = do.kind(1)
                do.h(3)
                do.pre(0)
                do.suf(0)
                do.h(4)
                do.score_cols(0)
                do.arg(0, at0)
                do.h(5)
                do.pre(1)
                do.suf(1)
                do.h(6)
                do.score_cols(1)
                do.h(7)
                do.arg(1, at1)
            do.lowrep(0)
            if tail is LAST:
                dve_last(eng, do, at0, at1)
                return
            if tail:
                do.rowsum(0)
                do.rowsum(1)
                do.x2(0, at0)
            do.lowrep(1)
            if not tail:
                do.w2(E - 2)
            if tail:
                do.x2(1, at1)
            if tail:
                do.ut(0)
            do.lt(0)
            do.lowrep(2)
            do.x1(0)
            do.x1(1)
            if tail:
                do.ut(1)
                do.out(0)
            dve_x0t(eng, i + 1, 0)
            dve_x0t(eng, i + 1, 1)
            do.lowrep(3)
            do.lt(1)
            do.x1(2)
            do.x1(3)
            dve_low(eng, i + 1)
            if not tail:
                do.w2(E - 1)
            if tail:
                do.out(1)

        def dve_last(eng, do, do_at0, do_at1):
            last = dve_steps(eng, PAIRS - 1, PAIRS - 1, LAST)
            do.rowsum(0)
            do.rowsum(1)
            last.lowrep(1)
            last.lt(0)
            last.x1(0)
            last.x1(1)
            last.lowrep(2)
            at0 = last.kind(0)
            last.x1t(0)
            last.lowrep(3)
            at1 = last.kind(1)
            last.tstk(0)
            last.lt(1)
            last.x1(2)
            last.x1(3)
            do.x2(0, do_at0)
            last.pre(0)
            last.suf(0)
            last.x1t(1)
            last.score_cols(0)
            do.x2(1, do_at1)
            last.tstk(1)
            last.arg(0, at0)
            do.ut(0)
            last.pre(1)
            last.suf(1)
            last.score_cols(1)
            last.arg(1, at1)
            last.tt(0)
            last.tt(1)
            do.ut(1)
            last.p_lo(1)
            last.x2(0, at0)
            do.out(0)
            last.x2_lo(0)
            last.x2(1, at1)
            do.out(1)
            last.x2_lo(1)
            last.ut(0)
            last.rowsum(0)
            last.rowsum(1)
            last.ut(1)
            last.out(0)
            last.out(1)

        def dve_low(eng, i):
            eng.wait_ge(s["act_low"], i + 1)
            q = slice(4 * R, P)
            minus(low[q], hbank[1][q, :], low[q]).then_inc(s["dve_low"], 1)

        def dve_prologue(eng):
            def side_by_side(dst, src, n):
                nc.vector.tensor_copy(dst[:].rearrange("p t (g r) -> p t g r", g=G),
                                      src[:].rearrange("p (t o r) -> p t o r", o=1, r=R).to_broadcast([P, n, G, R])
                                      ).then_inc(s["cib_ok" if src is cib_raw else "cob_ok"], 1)

            eng.wait_ge(s["cib_in"], 16)
            side_by_side(cib_s, cib_raw, FT)
            low_half = slice(P // 2, P)
            quadrants = [slice(P // 4, P // 2), slice(3 * P // 4, P)]
            eng.wait_ge(s["act_cia"], 1)
            for q in quadrants:
                m = minus(cia_st[q], cia_raw[q], cia_st[q])
            m.then_inc(s["dve_cia"], 1)
            for a in range(2):
                eng.wait_ge(s["act_cib"], 1 + a)
                dst = cibT[low_half].rearrange("r (n t) -> r t n", t=FT)[:, 4 * a:4 * a + 4]
                minus(dst, obank[a][low_half, :].rearrange("r (t n) -> r t n", t=4), dst).then_inc(s["dve_cib"], 1)
            for k in range(DT):
                eng.wait_ge(s["act_eia"], DT)
                src = mbank[0][:, k * P:(k + 1) * P].rearrange("p (e o r) -> p e o r", e=E, o=1)
                for c in (0, 4 * R):
                    hi, lo = (eia_st[:, :, k, c + n * 2 * R:c + (n + 1) * 2 * R].rearrange(
                        "p e (g r) -> p e g r", g=2) for n in range(2))
                    m = minus(lo, src.to_broadcast([P, E, 2, R]), hi)
                m.then_inc(s["dve_eia"], 1)
            eng.wait_ge(s["ewib_in"], 16)
            nc.vector.tensor_copy(ewib_s[:].rearrange("p t (e r) -> p t e r", r=R),
                                  ewib_raw[:].rearrange("p e (t r) -> p t e r", r=R)).then_inc(s["ewib_ok"], 1)
            for n, bank in enumerate(WI_BANKS):
                k, a = divmod(n, 2)
                eng.wait_ge(s["act_wi"], 1 + n)
                c = slice(a * 512, (a + 1) * 512)
                minus(wiT_l[:, k, c], bank[:, :], wiT_h[:, k, c]).then_inc(s["dve_wi"], 1)
                if n == 2:
                    eng.wait_ge(s["act_cob"], 1)
                    dst = cobT[low_half].rearrange("r (n t) -> r t n", t=DT)
                    minus(dst, obank[0][low_half, 0:D].rearrange("r (t n) -> r t n", t=DT), dst).then_inc(s["dve_cob"], 1)
                if n == 0:
                    eng.wait_ge(s["cob_in"], 16)
                    side_by_side(cob_s, cob_raw, DT)
                if n == 1:
                    for a in range(2):
                        eng.wait_ge(s["act_eib"], 1 + a)
                        hi, lo = (eib_st[:, h].rearrange("p (n t) -> p t n", t=FT)[:, 4 * a:4 * a + 4]
                                  for h in range(2))
                        nc.vector.scalar_tensor_tensor(
                            out=lo, in0=hbank[a][:, :].rearrange("p (t n) -> p t n", t=4), scalar=ALPHA,
                            in1=hi.bitcast(F32), op0=ALU.mult, op1=ALU.subtract).then_inc(s["dve_eib"], 1)
                    eng.wait_ge(s["act_coa"], 1)
                    q = quadrants[1]
                    minus(coa_st[q], coa_raw[q], coa_st[q]).then_inc(s["dve_coa"], 1)
            dve_x0t(eng, 0, 0)
            dve_x0t(eng, 0, 1)
            eng.wait_ge(s["ewob_in"], 16)
            nc.vector.tensor_copy(ewob_s[:].rearrange("p t (e r) -> p t e r", r=R),
                                  ewob_raw[:].rearrange("p e (t r) -> p t e r", r=R)).then_inc(s["ewob_ok"], 1)
            for n, bank in enumerate(WO_BANKS):
                eng.wait_ge(s["act_wo"], 1 + n)
                c = slice(2 * n, 2 * n + 2)
                minus(woT_l[:, c, R:R + D], bank[:, :].rearrange("p (a n) -> p a n", a=2),
                      woT_h[:, c, R:R + D]).then_inc(s["dve_wo"], 1)
            dve_low(eng, 0)
            eng.wait_ge(s["act_eob"], 1)
            hi, lo = (eob_st[:, n].rearrange("p (n t) -> p t n", t=DT) for n in range(2))
            nc.vector.scalar_tensor_tensor(
                out=lo, in0=obank[0][:, 0:D].rearrange("p (t n) -> p t n", t=DT), scalar=ALPHA,
                in1=hi.bitcast(F32), op0=ALU.mult, op1=ALU.subtract).then_inc(s["dve_eob"], 1)
            for a, bank in enumerate(EOA_BANKS):
                eng.wait_ge(s["act_eoa"], 1 + a)
                minus(ewoT_l[:, 4 * a:4 * a + 4], bank[:, :].rearrange("p (t n) -> p t n", t=4),
                      ewoT_h[:, 4 * a:4 * a + 4]).then_inc(s["dve_eoa"], 1)

        def dve_tables():
            eng = nc.vector
            eng.wait_ge(s["small_in"], 80)
            w1 = w1_raw[:].rearrange("p k (o a) -> p k o a", o=1).to_broadcast([P, DT, 2, A])
            w1h, w1l = (t[:].rearrange("p k (o a) -> p k o a", o=2) for t in (w1_h, w1_l))
            nc.vector.tensor_copy(w1h, w1).then_inc(s["small_ok"], 1)
            nc.vector.tensor_copy(v_h[:], v_c[:].to_broadcast([P, P])).then_inc(s["small_ok"], 1)
            eng.wait_ge(s["small_ok"], 2)
            minus(w1l, w1, w1h).then_inc(s["small_ok"], 1)
            minus(v_l[:], v_c[:].to_broadcast([P, P]), v_h[:]).then_inc(s["small_ok"], 1)
            eng.wait_ge(s["masks_ok"], 3)
            eng.wait_ge(s["cnt_ok"], 3)
            nc.vector.tensor_copy(cnt[:], cnt_i[:]).then_inc(s["cnt_ok"], 1)
            eng.wait_ge(s["cnt_ok"], 4)
            eng.wait_ge(s["ids_in"], 48)
            eng.sem_inc(s["dve_out"], 1)

        def minus_pool(dst, src, hi):
            return nc.gpsimd.tensor_tensor(dst, src, hi.bitcast(F32), ALU.subtract)

        def pool_prologue(eng):
            eng.memset(ident[:], 0.0).then_inc(s["ident_ok"], 1)
            eng.wait_ge(s["ident_ok"], 1)
            eng.affine_select(out=ident[:], in_=ident[:], compare_op=ALU.not_equal, fill=1.0, base=0,
                              pattern=[[-1, P]], channel_multiplier=1).then_inc(s["ident_ok"], 1)
            for k, (a, b) in enumerate(((S + 1, S + 1), (0, 0), (S, 1))):
                eng.memset(pre_at[0:1, k:k + 1], a)
                eng.memset(suf_at[0:1, k:k + 1], b)
            eng.memset(pre_max[:, 0:S + 1], -BIG)
            eng.memset(suf_max[:, S:], -BIG)
            eng.memset(mask_big[:], 0.0).then_inc(s["masks_ok"], 1)
            eng.iota(cnt_i[:, 0], pattern=[[P, ST]], base=1, channel_multiplier=1).then_inc(s["cnt_ok"], 1)
            eng.iota(cnt_i[:, 1], pattern=[[-P, ST]], base=S, channel_multiplier=-1).then_inc(s["cnt_ok"], 1)
            eng.iota(cnt_i[:, 2], pattern=[[0, ST]], base=S - 1, channel_multiplier=0).then_inc(s["cnt_ok"], 1)
            eng.wait_ge(s["masks_ok"], 1)
            for k, (sign, op) in enumerate(((1, ALU.is_ge), (-1, ALU.is_ge), (1, ALU.not_equal))):
                m = eng.affine_select(out=mask_big[:, k], in_=mask_big[:, k], compare_op=op, fill=BIG, base=0,
                                      pattern=[[-sign * P, ST], [sign, S]], channel_multiplier=-sign)
            m.then_inc(s["masks_ok"], 2)
            eng.wait_ge(s["act_coa"], 1)
            eng.wait_ge(s["masks_ok"], 3)
            q = slice(P // 4, P // 2)
            minus_pool(coa_st[q], coa_raw[q], coa_st[q]).then_inc(s["pool_coa"], 1)
            eng.wait_ge(s["pool_coa"], 1)
            eng.wait_ge(s["ids_in"], 48)
            eng.wait_ge(s["dve_eia"], DT)
            for j in range(2):
                e = eng.value_load(ids[0:1, 0, j:j + 1], min_val=0, max_val=E - 1)
                nc.gpsimd.tensor_copy(eia[:, j:j + 1], eia_st[:, bass.ds(e, 1)].bitcast(F32)
                                      ).then_inc(s["eia_in"], 16)
            pool_w2(eng, 0)

        def pool_w2(eng, half):
            eng.wait_ge(s[f"w2_in{half}"], 16)
            for e in range(half * E // 2, (half + 1) * E // 2):
                for t in range(DT):
                    d = w2_raw[:, e, t, t * P:(t + 1) * P]
                    m = nc.gpsimd.tensor_tensor(d, d, ident[:], ALU.add)
                m.then_inc(s["w2_ok"], 1)

        def pool_t(eng, p):
            eng.wait_ge(s["t_in"], 32 * (p + 1))
            for j in range(2):
                for t in range(ST):
                    d = t_raw[:, j, t, t * P:(t + 1) * P]
                    nc.gpsimd.tensor_tensor(d, d, ident[:], ALU.add).then_inc(s["pool_ti"], 1)

        def pool_x1(eng, p, j, at):
            eng.wait_ge(s["act_x1h"], 2 * p + j + 1)
            minus_pool(x1_l[:, j, :, 0:D], at.x1[:, j], x1_h[:, j, :, 0:D]).then_inc(s["pool_x1l"], 1)

        def pool_p(eng, p, j):
            eng.wait_ge(s["act_ph"], 2 * p + j + 1)
            minus_pool(p_l[:, j], terms[:, j], p_h[:, j]).then_inc(s["p_lo"], 1)

        def pool_x2(eng, p, j):
            eng.wait_ge(s["act_x2h"], 2 * p + j + 1)
            minus_pool(x2_l[:, j], x2[:, j], x2_h[:, j]).then_inc(s["x2_lo"], 1)

        def pool_body(eng, i, tail):
            p = i - 1
            if not tail:
                eng.wait_ge(s["dve_eoa"], 2)
            if tail:
                pool_t(eng, p)
                pool_x1(eng, p, 0, STEADY)
                pool_x1(eng, p, 1, STEADY)
            for j in range(2):
                e = eng.value_load(ids[0:1, 0, bass.ds(2 * i + j, 1)], min_val=0, max_val=E - 1)
                if j == 0 and tail:
                    eng.wait_ge(s["pe_o"], 4 * i)
                c = slice(j * (R + D), j * (R + D) + R)
                for src, dst in ((ewoT_h, woT_h), (ewoT_l, woT_l)):
                    nc.gpsimd.tensor_copy(dst[:, :, c], src[:, :, bass.ds(e * R, R)].bitcast(F32)
                                          ).then_inc(s["pool_eoa"], 1)
            if not tail:
                pool_w2(eng, 1)
                eng.wait_ge(s["pe_w2"], E)
                eng.memset(x1_h[:, :, :, D:].bitcast(F32), 1.0).then_inc(s["ones_ok"], 1)
                eng.memset(x1_l[:, :, :, D:].bitcast(F32), 0.0).then_inc(s["ones_ok"], 1)
            if tail:
                pool_p(eng, p, 0)
                pool_p(eng, p, 1)
            if tail is LAST:
                pool_t(eng, p + 1)
            if tail:
                pool_x2(eng, p, 0)
            if tail is LAST:
                pool_x1(eng, p + 1, 0, LAST)
            if tail:
                pool_x2(eng, p, 1)
            if tail is LAST:
                pool_x1(eng, p + 1, 1, LAST)
                pool_p(eng, p + 1, 0)

        def run(eng, prologue, body):
            prologue(eng)
            body(eng, 0, None)
            with eng.Fori(1, PAIRS - 1) as i:
                body(eng, i, STEADY)
            body(eng, PAIRS - 1, LAST)

        block = ctx.enter_context(nc.Block())

        @block.sync
        def _(eng):
            run(eng, sp_prologue, sp_body)
            eng.wait_ge(s["out_free"], 32 * PAIRS + 32)

        @block.tensor
        def _(eng):
            run(eng, pe_prologue, pe_body)

        @block.scalar
        def _(eng):
            run(eng, act_prologue, act_body)

        @block.vector
        def _(eng):
            run(eng, dve_prologue, dve_body)

        @block.gpsimd
        def _(eng):
            run(eng, pool_prologue, pool_body)


_INS = ['x', 'itok_B_0_7', 'itok_B_0_2', 'itok_B_1_98', 'L0_cond_wi', 'L0_cond_wo', 'L0_cond_common_wi_a',
        'L0_cond_common_wi_b', 'L0_cond_common_wo_a', 'L0_cond_common_wo_b', 'L0_cond_experts_wi_a',
        'L0_cond_experts_wi_b', 'L0_cond_experts_wo_a', 'L0_cond_experts_wo_b', 'L1_cond_W1', 'L1_cond_b1',
        'L1_cond_v', 'L2_cond_weight', 'L2_cond_bias', 'L3_cond_T']


def kernel(**inputs):
    import numpy as _np
    import concourse.bacc as _bacc
    from concourse import mybir as _mybir
    from concourse.bass_utils import run_bass_kernel_spmd as _run

    nc = _bacc.Bacc("TRN2", target_bir_lowering=False, num_devices=1)
    arrays, args = {}, []
    for name in _INS:
        a = _np.ascontiguousarray(inputs[name])
        arrays[f"in_{name}_dram"] = a
        args.append(nc.dram_tensor(f"in_{name}_dram", a.shape, _mybir.dt.from_np(a.dtype), kind="ExternalInput").ap())
    shape = arrays["in_x_dram"].shape
    args.append(nc.dram_tensor("out_0_dram", shape, _mybir.dt.from_np(_np.dtype("float32")), kind="ExternalOutput").ap())
    build(nc, *args)
    r = _run(nc, [arrays], core_ids=[0])
    return r.results[0]["out_0_dram"]
```
